# Optimizing a Trainium2 kernel written in Bass

```python
import numpy as np
import jax
import jax.numpy as jnp

def _softmax(x, axis=-1):
    return jax.nn.softmax(x, axis=axis)

def _gelu(x):
    return jax.nn.gelu(x, approximate=True)

def _silu(x):
    return jax.nn.silu(x)

def _sigmoid(x):
    return jax.nn.sigmoid(x)

def _layernorm(x, axis=-1, eps=1e-05):
    m = jnp.mean(x, axis=axis, keepdims=True)
    v = jnp.var(x, axis=axis, keepdims=True)
    return (x - m) / jnp.sqrt(v + eps)

def _scatter_add(tgt, idx, src, axis=0):
    return tgt.at[idx].add(src)

def _segment_sum(src, seg, n):
    return jax.ops.segment_sum(src, seg, n)
kernel_name = 'mk_prb_d1_jaxref_r8_e82708'

def setup_inputs(seed: int=0):
    np.random.seed(seed)
    _w = jnp.asarray

    def _L0_attn_setup():
        import jax, jax.numpy as jnp
        import numpy as np
        import math
        N_HEAD = 16
        ROPE_BASE = 10000.0

        def _rope_cos_sin(seq_len, head_dim, dtype):
            half = head_dim // 2
            inv_freq = ROPE_BASE ** (-(jnp.arange(half, dtype=jnp.float32) * 2.0 / head_dim))
            t = jnp.arange(seq_len, dtype=jnp.float32)
            ang = t[:, None] * inv_freq[None, :]
            return (jnp.cos(ang).astype(dtype), jnp.sin(ang).astype(dtype))

        def _apply_rope(x, cos, sin):
            x1 = x[..., 0::2]
            x2 = x[..., 1::2]
            c = cos[None, :, None, :]
            s = sin[None, :, None, :]
            out = jnp.stack([x1 * c - x2 * s, x1 * s + x2 * c], axis=-1)
            return out.reshape(x.shape)
        key = jax.random.key(seed)
        kx, kq, kk, kv, ko = jax.random.split(key, 5)
        B, S, H = (2, 256, 128)
        x = jax.random.normal(kx, (B, S, H), dtype=jnp.float32)
        scale = 0.02
        w_q = jax.random.normal(kq, (H, H), dtype=jnp.float32) * scale
        w_k = jax.random.normal(kk, (H, H), dtype=jnp.float32) * scale
        w_v = jax.random.normal(kv, (H, H), dtype=jnp.float32) * scale
        w_o = jax.random.normal(ko, (H, H), dtype=jnp.float32) * scale
        return {'x': x, 'w_q': w_q, 'w_k': w_k, 'w_v': w_v, 'w_o': w_o}
    _L0_attn_in = _L0_attn_setup()

    def _L0_ffn_setup():
        import jax, jax.numpy as jnp
        import numpy as np
        DIM = 128
        DEPTH = 6
        HEADS = 16
        DIM_HEAD = 64
        WINDOW = 32
        INNER = HEADS * DIM_HEAD
        DIM_INNER = int(DIM * 4 * 2 / 3)
        QK_SCALE = 8.0

        def shift_tokens(t):
            a, s = jnp.split(t, 2, -1)
            s = jnp.pad(s, ((0, 0), (1, 0), (0, 0)))[:, :-1]
            return jnp.concatenate([a, s], -1)

        def l2norm(t):
            return t / jnp.maximum(jnp.linalg.norm(t, axis=-1, keepdims=True), 1e-12)

        def rotate_half(x):
            x1, x2 = jnp.split(x, 2, -1)
            return jnp.concatenate([-x2, x1], -1)

        def rotary_tables(n):
            half = jnp.arange(0, DIM_HEAD, 2, dtype=jnp.float32)
            inv_freq = 1.0 / 10000.0 ** (half / DIM_HEAD)
            t = jnp.arange(n, dtype=jnp.float32)
            freqs = t[:, None] * inv_freq[None, :]
            freqs = jnp.concatenate([freqs, freqs], -1)
            base_scale = (half + 0.4 * DIM_HEAD) / (1.4 * DIM_HEAD)
            power = (t - n // 2) / (WINDOW // 2)
            scale = base_scale[None, :] ** power[:, None]
            scale = jnp.concatenate([scale, scale], -1)
            return (freqs, scale)

        def local_attention(q, k, v):
            b, h, n, d = q.shape
            w = WINDOW
            nw = n // w
            bq = q.reshape(b, h, nw, w, d)
            bk = k.reshape(b, h, nw, w, d)
            bv = v.reshape(b, h, nw, w, d)

            def look(t):
                p = jnp.pad(t, ((0, 0), (0, 0), (1, 0), (0, 0), (0, 0)))
                return jnp.concatenate([p[:, :, :nw], p[:, :, 1:]], axis=3)
            bk2, bv2 = (look(bk), look(bv))
            seq = jnp.arange(n).reshape(nw, w)
            seq_p = jnp.pad(seq, ((1, 0), (0, 0)), constant_values=-1)
            jt = jnp.concatenate([seq_p[:nw], seq_p[1:]], axis=1)
            it = seq[:, :, None]
            jb = jt[:, None, :]
            mask = (it < jb) | (it > jb + w) | (jb == -1)
            sim = jnp.einsum('bhwie,bhwje->bhwij', bq, bk2) * QK_SCALE
            sim = jnp.where(mask, -jnp.finfo(sim.dtype).max, sim)
            attn = jax.nn.softmax(sim, -1)
            out = jnp.einsum('bhwij,bhwje->bhwie', attn, bv2)
            return out.reshape(b, h, n, d)

        def attn_layer(x, Wqkv, qs, ksc, Wo):
            b, n, _ = x.shape
            qkv = x @ Wqkv
            q, k, v = jnp.split(qkv, 3, -1)
            sh = lambda t: t.reshape(b, n, HEADS, DIM_HEAD).transpose(0, 2, 1, 3)
            q, k, v = (sh(q), sh(k), sh(v))
            q = l2norm(q) * qs
            k = l2norm(k) * ksc
            freqs, scale = rotary_tables(n)
            cos, sin = (jnp.cos(freqs), jnp.sin(freqs))
            q = q * cos * scale + rotate_half(q) * sin * scale
            inv = 1.0 / scale
            k = k * cos * inv + rotate_half(k) * sin * inv
            out = local_attention(q, k, v)
            out = out.transpose(0, 2, 1, 3).reshape(b, n, INNER)
            return out @ Wo

        def ffn_layer(x, g, bln, W1, b1, W2, b2):
            mu = x.mean(-1, keepdims=True)
            var = ((x - mu) ** 2).mean(-1, keepdims=True)
            xn = (x - mu) / jnp.sqrt(var + 1e-05) * g + bln
            hg = xn @ W1 + b1
            a, gate = jnp.split(hg, 2, -1)
            return a * jax.nn.gelu(gate, approximate=False) @ W2 + b2
        key = jax.random.key(seed)
        ks = jax.random.split(key, 8)
        B, N = (2, 256)
        init = lambda k, shape: jax.random.normal(k, shape, jnp.float32) * 0.02
        return {'x': jax.random.normal(ks[0], (B, N, DIM), jnp.float32), 'Wqkv': init(ks[1], (DEPTH, DIM, 3 * INNER)), 'q_scale': jnp.ones((DEPTH, DIM_HEAD), jnp.float32), 'k_scale': jnp.ones((DEPTH, DIM_HEAD), jnp.float32), 'Wo': init(ks[2], (DEPTH, INNER, DIM)), 'ln_g': jnp.ones((DEPTH, DIM), jnp.float32), 'ln_b': jnp.zeros((DEPTH, DIM), jnp.float32), 'W1': init(ks[3], (DEPTH, DIM, 2 * DIM_INNER)), 'b1': jnp.zeros((DEPTH, 2 * DIM_INNER), jnp.float32), 'W2': init(ks[4], (DEPTH, DIM_INNER, DIM)), 'b2': jnp.zeros((DEPTH, DIM), jnp.float32)}
    _L0_ffn_in = _L0_ffn_setup()
    _d = {'L0_attn_x': _L0_attn_in['x'], 'L0_attn_w_q': _L0_attn_in['w_q'], 'L0_attn_w_k': _L0_attn_in['w_k'], 'L0_attn_w_v': _L0_attn_in['w_v'], 'L0_attn_w_o': _L0_attn_in['w_o'], 'L0_ffn_Wqkv': _L0_ffn_in['Wqkv'], 'L0_ffn_q_scale': _L0_ffn_in['q_scale'], 'L0_ffn_k_scale': _L0_ffn_in['k_scale'], 'L0_ffn_Wo': _L0_ffn_in['Wo'], 'L0_ffn_ln_g': _L0_ffn_in['ln_g'], 'L0_ffn_ln_b': _L0_ffn_in['ln_b'], 'L0_ffn_W1': _L0_ffn_in['W1'], 'L0_ffn_b1': _L0_ffn_in['b1'], 'L0_ffn_W2': _L0_ffn_in['W2'], 'L0_ffn_b2': _L0_ffn_in['b2']}
    _x0 = _d['L0_attn_x']
    _d['L0_attn_x'] = jax.random.normal(jax.random.fold_in(jax.random.key(seed), 1), (4, 1024, 128), dtype=_x0.dtype)
    del _x0
    return _d

def reference(L0_attn_x, L0_attn_w_q, L0_attn_w_k, L0_attn_w_v, L0_attn_w_o, L0_ffn_Wqkv, L0_ffn_q_scale, L0_ffn_k_scale, L0_ffn_Wo, L0_ffn_ln_g, L0_ffn_ln_b, L0_ffn_W1, L0_ffn_b1, L0_ffn_W2, L0_ffn_b2):

    def _L0_attn_ref(x, w_q, w_k, w_v, w_o):
        import jax, jax.numpy as jnp
        import numpy as np
        import math
        N_HEAD = 16
        ROPE_BASE = 10000.0

        def _rope_cos_sin(seq_len, head_dim, dtype):
            half = head_dim // 2
            inv_freq = ROPE_BASE ** (-(jnp.arange(half, dtype=jnp.float32) * 2.0 / head_dim))
            t = jnp.arange(seq_len, dtype=jnp.float32)
            ang = t[:, None] * inv_freq[None, :]
            return (jnp.cos(ang).astype(dtype), jnp.sin(ang).astype(dtype))

        def _apply_rope(x, cos, sin):
            x1 = x[..., 0::2]
            x2 = x[..., 1::2]
            c = cos[None, :, None, :]
            s = sin[None, :, None, :]
            out = jnp.stack([x1 * c - x2 * s, x1 * s + x2 * c], axis=-1)
            return out.reshape(x.shape)
        B, S, H = x.shape
        d = H // N_HEAD
        q = (x @ w_q.T).reshape(B, S, N_HEAD, d)
        k = (x @ w_k.T).reshape(B, S, N_HEAD, d)
        v = (x @ w_v.T).reshape(B, S, N_HEAD, d)
        cos, sin = _rope_cos_sin(S, d, x.dtype)
        q = _apply_rope(q, cos, sin)
        k = _apply_rope(k, cos, sin)
        scores = jnp.einsum('bqhd,bkhd->bhqk', q, k) / math.sqrt(d)
        coefs = jax.nn.softmax(scores, axis=-1)
        causal = jnp.tril(jnp.ones((S, S), dtype=bool))
        coefs = jnp.where(causal[None, None], coefs, 0.0)
        out = jnp.einsum('bhqk,bkhd->bqhd', coefs, v).reshape(B, S, H)
        return out @ w_o.T

    def _L0_ffn_ref(x, Wqkv, q_scale, k_scale, Wo, ln_g, ln_b, W1, b1, W2, b2):
        import jax, jax.numpy as jnp
        import numpy as np
        DIM = 128
        DEPTH = 6
        HEADS = 16
        DIM_HEAD = 64
        WINDOW = 32
        INNER = HEADS * DIM_HEAD
        DIM_INNER = int(DIM * 4 * 2 / 3)
        QK_SCALE = 8.0

        def shift_tokens(t):
            a, s = jnp.split(t, 2, -1)
            s = jnp.pad(s, ((0, 0), (1, 0), (0, 0)))[:, :-1]
            return jnp.concatenate([a, s], -1)

        def l2norm(t):
            return t / jnp.maximum(jnp.linalg.norm(t, axis=-1, keepdims=True), 1e-12)

        def rotate_half(x):
            x1, x2 = jnp.split(x, 2, -1)
            return jnp.concatenate([-x2, x1], -1)

        def rotary_tables(n):
            half = jnp.arange(0, DIM_HEAD, 2, dtype=jnp.float32)
            inv_freq = 1.0 / 10000.0 ** (half / DIM_HEAD)
            t = jnp.arange(n, dtype=jnp.float32)
            freqs = t[:, None] * inv_freq[None, :]
            freqs = jnp.concatenate([freqs, freqs], -1)
            base_scale = (half + 0.4 * DIM_HEAD) / (1.4 * DIM_HEAD)
            power = (t - n // 2) / (WINDOW // 2)
            scale = base_scale[None, :] ** power[:, None]
            scale = jnp.concatenate([scale, scale], -1)
            return (freqs, scale)

        def local_attention(q, k, v):
            b, h, n, d = q.shape
            w = WINDOW
            nw = n // w
            bq = q.reshape(b, h, nw, w, d)
            bk = k.reshape(b, h, nw, w, d)
            bv = v.reshape(b, h, nw, w, d)

            def look(t):
                p = jnp.pad(t, ((0, 0), (0, 0), (1, 0), (0, 0), (0, 0)))
                return jnp.concatenate([p[:, :, :nw], p[:, :, 1:]], axis=3)
            bk2, bv2 = (look(bk), look(bv))
            seq = jnp.arange(n).reshape(nw, w)
            seq_p = jnp.pad(seq, ((1, 0), (0, 0)), constant_values=-1)
            jt = jnp.concatenate([seq_p[:nw], seq_p[1:]], axis=1)
            it = seq[:, :, None]
            jb = jt[:, None, :]
            mask = (it < jb) | (it > jb + w) | (jb == -1)
            sim = jnp.einsum('bhwie,bhwje->bhwij', bq, bk2) * QK_SCALE
            sim = jnp.where(mask, -jnp.finfo(sim.dtype).max, sim)
            attn = jax.nn.softmax(sim, -1)
            out = jnp.einsum('bhwij,bhwje->bhwie', attn, bv2)
            return out.reshape(b, h, n, d)

        def attn_layer(x, Wqkv, qs, ksc, Wo):
            b, n, _ = x.shape
            qkv = x @ Wqkv
            q, k, v = jnp.split(qkv, 3, -1)
            sh = lambda t: t.reshape(b, n, HEADS, DIM_HEAD).transpose(0, 2, 1, 3)
            q, k, v = (sh(q), sh(k), sh(v))
            q = l2norm(q) * qs
            k = l2norm(k) * ksc
            freqs, scale = rotary_tables(n)
            cos, sin = (jnp.cos(freqs), jnp.sin(freqs))
            q = q * cos * scale + rotate_half(q) * sin * scale
            inv = 1.0 / scale
            k = k * cos * inv + rotate_half(k) * sin * inv
            out = local_attention(q, k, v)
            out = out.transpose(0, 2, 1, 3).reshape(b, n, INNER)
            return out @ Wo

        def ffn_layer(x, g, bln, W1, b1, W2, b2):
            mu = x.mean(-1, keepdims=True)
            var = ((x - mu) ** 2).mean(-1, keepdims=True)
            xn = (x - mu) / jnp.sqrt(var + 1e-05) * g + bln
            hg = xn @ W1 + b1
            a, gate = jnp.split(hg, 2, -1)
            return a * jax.nn.gelu(gate, approximate=False) @ W2 + b2
        for i in range(DEPTH):
            x = attn_layer(shift_tokens(x), Wqkv[i], q_scale[i], k_scale[i], Wo[i]) + x
            x = ffn_layer(shift_tokens(x), ln_g[i], ln_b[i], W1[i], b1[i], W2[i], b2[i]) + x
        return x
    x = L0_attn_x
    xn = _layernorm(x, axis=-1)
    x = x + _L0_attn_ref(xn, L0_attn_w_q, L0_attn_w_k, L0_attn_w_v, L0_attn_w_o) + _L0_ffn_ref(xn, L0_ffn_Wqkv, L0_ffn_q_scale, L0_ffn_k_scale, L0_ffn_Wo, L0_ffn_ln_g, L0_ffn_ln_b, L0_ffn_W1, L0_ffn_b1, L0_ffn_W2, L0_ffn_b2)
    return x

_drawn_inputs = setup_inputs


def setup_inputs(seed=0):
    import zlib

    import numpy as np

    out = dict(_drawn_inputs(seed))
    spreads = {'L0_ffn_q_scale': (1.0, 0.6),
     'L0_ffn_k_scale': (1.0, 0.6),
     'L0_ffn_ln_g': (1.0, 0.6),
     'L0_ffn_ln_b': (0.0, 0.8),
     'L0_ffn_b1': (0.0, 0.8),
     'L0_ffn_b2': (0.0, 0.1)}
    factors = {'L0_attn_w_q': 8.0,
     'L0_attn_w_k': 8.0,
     'L0_attn_w_v': 8.0,
     'L0_attn_w_o': 8.0,
     'L0_ffn_W1': 3.639,
     'L0_ffn_W2': 3.574}
    for name, (base, spread) in spreads.items():
        noise = np.random.default_rng([zlib.crc32(name.encode()), seed]).standard_normal(out[name].shape)
        drawn = base * np.exp(spread * noise) if base else spread * noise
        out[name] = jnp.asarray(drawn.astype(out[name].dtype))
    for name, factor in factors.items():
        out[name] = (out[name] * factor).astype(out[name].dtype)
    return out
```

```python
import numpy as np
import concourse.bass as bass
from concourse import mybir
from contextlib import ExitStack

F32 = mybir.dt.float32
BF16 = mybir.dt.bfloat16
ACT = mybir.ActivationFunctionType
ALU = mybir.AluOpType
AX = mybir.AxisListType

B, S, D = 4, 1024, 128
P = 128
T = S // P
CH = 512
C = S // CH
HA, DA = 16, 8
SCALE_A = 1.0 / float(np.sqrt(DA))
TERMS_Q = [0, 0, 1, 1, 0, 2]
TERMS_K = [0, 1, 0, 1, 2, 0]
SHIFT_ROW = 96
EPS = 1e-5
L, HB, DB, WIN = 6, 16, 64, 32
NP = HB // 2
SPAN = P + WIN
DI = 341
NJ = 3
DIP = NJ * P
HALF = DB
EXP_LN_SET = "natural_log_exp_and_others"
CONSTS = 4 * P + 3 * SPAN
ITEMS = 14
DVE_ITEMS = (0, 1, 2, 3, 4, 5, 6, 7, 10, 11, 12, 13)
ACT_ITEMS = (0, 2, 4, 6, 8, 9)
ND, NA = len(DVE_ITEMS), len(ACT_ITEMS)


def upto(items, n):
    return sum(i <= n for i in items)


def branch_a(nc, x, wA, cA, ident_d, causal_d, o_scr, xnt_scr, part_scr, m_scr):
    with ExitStack() as ctx:
        sb = lambda n, s, d=F32: ctx.enter_context(nc.sbuf_tensor(n, s, d))
        ps = lambda n: ctx.enter_context(nc.psum_tensor(n, [P, S], F32))
        sem = lambda n: ctx.enter_context(nc.semaphore(n))
        ident = sb("a_ident", [P, P])
        w = sb("a_w", [P, 5 * D])
        causal = sb("a_causal", [P, P])
        rope = sb("a_rope", [P, 2, S])
        xtok = sb("a_xtok", [P, T, D])
        xc = sb("a_xc", [P, T, D])
        sq = sb("a_sq", [P, T, D])
        mean, var, rstd = sb("a_mean", [P, T]), sb("a_var", [P, T]), sb("a_rstd", [P, T])
        std = sb("a_std", [P, T])
        xn = sb("a_xn", [P, T, D])
        xnt = sb("a_xnt", [P, S])
        cosq = sb("a_cosq", [P, 2, S])
        sinq = sb("a_sinq", [P, 2, S])
        rest = sb("a_rest", [P, 2, S])
        parts = sb("a_parts", [P, 2, 3, S], BF16)
        v = sb("a_v", [P, T, D])
        qs = sb("a_qstack", [P, HA * S], BF16)
        ks = sb("a_kstack", [P, HA * S], BF16)
        negm = sb("a_negm", [P, HA * T])
        negmt = sb("a_negmt", [P, P], BF16)
        vh = sb("a_vh", [P, T, 32])
        ones = sb("a_ones", [P, 32])
        prob = sb("a_prob", [P, 4, S])
        diag = sb("a_diag", [P, 2, P])
        rec = sb("a_rec", [64, 2, CH])
        oh = sb("a_oh", [64, 2, CH])
        banks = [ps(f"a_ps{i}") for i in range(4)]

        const_in, w_in = sem("a_const_in"), sem("a_w_in")
        x_in, xnt_saved = sem("a_x_in"), sem("a_xnt_saved")
        zeroed = sem("a_zeroed")
        ln = sem("a_ln")
        std_done = sem("a_std_done")
        transposed, xnt_ready = sem("a_transposed"), sem("a_xnt_ready")
        proj, rot = sem("a_proj"), sem("a_rot")
        v_proj, v_ready = sem("a_v_proj"), sem("a_v_ready")
        rotated = sem("a_rotated")
        split = sem("a_split")
        parts_out, stacks_in = sem("a_parts_out"), sem("a_stacks_in")
        guard, guard_max = sem("a_guard"), sem("a_guard_max")
        m_trans, m_ready = sem("a_m_trans"), sem("a_m_ready")
        m_out, m_in = sem("a_m_out"), sem("a_m_in")
        scored, exped, masked, summed = sem("a_scored"), sem("a_exped"), sem("a_masked"), sem("a_summed")
        vh_ready, recd = sem("a_vh_ready"), sem("a_recd")
        normed = [sem("a_normed0"), sem("a_normed1")]
        o_saved = [sem("a_o_saved0"), sem("a_o_saved1")]
        block = ctx.enter_context(nc.Block())
        NDMA_STACK = 16 * 2 * len(TERMS_Q)

        @block.sync
        def _(sp):
            for started in (xnt_saved, parts_out, m_out, o_saved[0], o_saved[1],):
                sp.nop().then_inc(started, 1)
            sp.dma_start(ident[:, :], ident_d).then_inc(const_in, 16)
            sp.dma_start(causal[:, :], causal_d).then_inc(const_in, 16)
            sp.dma_start(rope[:, :, :], cA).then_inc(const_in, 16)
            sp.dma_start(w[:, :], wA).then_inc(w_in, 16)
            with sp.Fori(0, B) as b:
                sp.wait_ge(ln, 1 + 7 * b)
                sp.dma_start(xtok[:, :, :], x[b].rearrange("(t p) d -> p t d", p=P)).then_inc(x_in, 16)
                sp.wait_ge(xnt_ready, b + 1)
                sp.dma_start(xnt_scr[b], xnt[:, :]).then_inc(xnt_saved, 16)
                for side in range(2):
                    sp.wait_ge(split, 6 * b + 5 + side)
                    sp.dma_start(part_scr[side].rearrange("t p n -> p t n"), parts[:, side, :, :]).then_inc(parts_out, 16)
                sp.wait_ge(parts_out, 1 + 32 * b + 32)
                sp.wait_ge(zeroed, 5)
                for stack, side, terms in ((qs, 0, TERMS_Q), (ks, 1, TERMS_K)):
                    for t, part in enumerate(terms):
                        sp.dma_start(stack[DA * t:DA * t + DA, :].rearrange("r (h n) -> r h n", h=HA),
                                     part_scr[side, part].rearrange("(h r) n -> r h n", r=DA)).then_inc(stacks_in, 16)
                sp.wait_ge(m_ready, b + 1)
                sp.dma_start(m_scr, negmt[:, :]).then_inc(m_out, 16)
                sp.wait_ge(m_out, 1 + 16 * b + 16)
                sp.dma_start(qs[SHIFT_ROW:SHIFT_ROW + 1, :], m_scr.rearrange("(a m) n -> a (m n)", a=1)).then_inc(m_in, 16)
                with sp.Fori(0, HA // 2) as hh:
                    for par in range(2):
                        g = b * (HA // 2) + hh
                        sp.wait_ge(normed[par], 1 + g + 1)
                        for c in range(C):
                            sp.dma_start(o_scr[b, bass.ds((2 * hh + par) * DA, DA), c * CH:(c + 1) * CH],
                                         oh[32 * c:32 * c + DA, par, :]).then_inc(o_saved[par], 16)
            sp.wait_ge(xnt_saved, 1 + 16 * B)
            for par in range(2):
                sp.wait_ge(o_saved[par], 1 + 32 * B * HA // 2)

        @block.gpsimd
        def _(pool):
            nc.gpsimd.memset(qs[:, :], 0.0).then_inc(zeroed, 1)
            nc.gpsimd.memset(ks[:, :], 0.0).then_inc(zeroed, 1)
            nc.gpsimd.memset(vh[:, :, :], 0.0).then_inc(zeroed, 1)
            nc.gpsimd.memset(ones[:, :], 1.0).then_inc(zeroed, 1)
            pool.wait_ge(zeroed, 4)
            pool.wait_ge(const_in, 48)
            nc.gpsimd.memset(ks[SHIFT_ROW:SHIFT_ROW + 1, :], 1.0).then_inc(zeroed, 1)
            pool.wait_ge(zeroed, 5)
            with pool.Fori(0, B) as b:
                for side in range(2):
                    pool.wait_ge(rot, 4 * b + 2 * side + 2)
                    nc.gpsimd.tensor_tensor(rest[:, side, :], cosq[:, side, :], sinq[:, side, :], ALU.add).then_inc(rotated, 1)
                for step in range(2):
                    for side in range(2):
                        pool.wait_ge(split, 6 * b + 2 * step + side + 1)
                        pool.wait_ge(rotated, 6 * b + 2 * step + side + 1)
                        nc.gpsimd.tensor_tensor(rest[:, side, :], rest[:, side, :], parts[:, side, step, :],
                                                ALU.subtract).then_inc(rotated, 1)
                with pool.Fori(0, HA) as h:
                    g = b * HA + h
                    pool.wait_ge(v_ready, b + 1)
                    pool.wait_ge(summed, 1 + 8 * g)
                    nc.gpsimd.tensor_copy(vh[:, :, 0:DA], v[:, :, bass.ds(h * DA, DA)]).then_inc(vh_ready, 1)
                    for kt in range(T):
                        pool.wait_ge(exped, 8 * g + kt + 1)
                        if kt >= 2:
                            pool.wait_ge(summed, 1 + 8 * g + kt - 1)
                        nc.gpsimd.tensor_tensor(diag[:, kt % 2, :], prob[:, kt % 4, kt * P:(kt + 1) * P], causal[:, :],
                                                ALU.mult).then_inc(masked, 1)

        @block.vector
        def _(dve):
            for started in (ln, guard_max, normed[0], normed[1],):
                dve.nop().then_inc(started, 1)
            with dve.Fori(0, B) as b:
                dve.wait_ge(x_in, 16 * b + 16)
                dve.wait_ge(transposed, 1 + b)
                n = 7 * b
                bc = lambda t: t[:, :].rearrange("p (t o) -> p t o", o=1).broadcast_to([P, T, D])
                nc.vector.tensor_reduce(mean[:, :], xtok[:, :, :], axis=AX.X, op=ALU.add).then_inc(ln, 1)
                dve.wait_ge(ln, 1 + n + 1)
                nc.vector.tensor_scalar(mean[:, :], mean[:, :], 1.0 / D, None, ALU.mult).then_inc(ln, 1)
                dve.wait_ge(ln, 1 + n + 2)
                nc.vector.tensor_tensor(xc[:, :, :], xtok[:, :, :], bc(mean), ALU.subtract).then_inc(ln, 1)
                dve.wait_ge(ln, 1 + n + 3)
                nc.vector.tensor_tensor(sq[:, :, :], xc[:, :, :], xc[:, :, :], ALU.mult).then_inc(ln, 1)
                dve.wait_ge(ln, 1 + n + 4)
                nc.vector.tensor_reduce(var[:, :], sq[:, :, :], axis=AX.X, op=ALU.add).then_inc(ln, 1)
                dve.wait_ge(ln, 1 + n + 5)
                nc.vector.tensor_scalar(var[:, :], var[:, :], 1.0 / D, EPS, ALU.mult, ALU.add).then_inc(ln, 1)
                dve.wait_ge(std_done, b + 1)
                nc.vector.reciprocal(rstd[:, :], std[:, :]).then_inc(ln, 1)
                dve.wait_ge(ln, 1 + n + 7)
                nc.vector.tensor_tensor(xn[:, :, :], xc[:, :, :], bc(rstd), ALU.mult).then_inc(recd, 1)
                dve.wait_ge(transposed, 1 + b + 1)
                dve.wait_ge(xnt_saved, 1 + 16 * b)
                nc.vector.tensor_copy(xnt[:, :], banks[0][:, :]).then_inc(xnt_ready, 1)
                dve.wait_ge(const_in, 48)
                for side in range(2):
                    for k, dst in ((0, cosq), (1, sinq)):
                        n4 = 2 * side + k
                        dve.wait_ge(proj, 8 * b + 2 * n4 + 2)
                        nc.vector.tensor_tensor(dst[:, side, :], banks[(n4 + 1) % 4][:, :], rope[:, k, :],
                                                ALU.mult).then_inc(rot, 1)
                with dve.Fori(0, HA) as h:
                    g = b * HA + h
                    for qt in range(T):
                        dve.wait_ge(guard, 8 * g + qt + 1)
                        nc.vector.tensor_reduce(negm[:, bass.ds(h * T + qt, 1)], banks[qt % 4][:, :], axis=AX.X,
                                                op=ALU.max, negate=True).then_inc(guard_max, 1)
                dve.wait_ge(m_trans, b + 1)
                dve.wait_ge(m_out, 1 + 16 * b)
                nc.vector.tensor_copy(negmt[:, :], banks[0][:, 0:P]).then_inc(m_ready, 1)
                with dve.Fori(0, HA // 2) as hh:
                    g = b * (HA // 2) + hh
                    for par in range(2):
                        acc = banks[2 + par]
                        dve.wait_ge(summed, 1 + 8 * (2 * g + par) + 8)
                        dve.wait_ge(normed[par], 1 + g)
                        nc.vector.reciprocal(rec[:, par, :], acc[64:128, 0:CH]).then_inc(recd, 1)
                        dve.wait_ge(recd, b + 2 * g + par + 2)
                        dve.wait_ge(o_saved[par], 1 + 32 * g)
                        nc.vector.tensor_tensor(oh[:, par, :], acc[0:64, 0:CH], rec[:, par, :], ALU.mult).then_inc(normed[par], 1)

        @block.scalar
        def _(act):
            with act.Fori(0, B) as b:
                act.wait_ge(ln, 1 + 7 * b + 6)
                nc.scalar.activation(std[:, :], var[:, :], ACT.Sqrt).then_inc(std_done, 1)
                nc.scalar.preload_act_table_set("exp_and_others")
                for part in range(3):
                    for side in range(2):
                        if part == 0:
                            act.wait_ge(parts_out, 1 + 32 * b)
                        act.wait_ge(rotated, 6 * b + 2 * part + side + 1)
                        nc.scalar.activation(parts[:, side, part, :], rest[:, side, :], ACT.Copy).then_inc(split, 1)
                act.wait_ge(v_proj, b + 1)
                nc.scalar.activation(v[:, :, :], banks[0][:, :].rearrange("p (t d) -> p t d", t=T), ACT.Copy).then_inc(v_ready, 1)
                with act.Fori(0, HA) as h:
                    g = b * HA + h
                    for kt in range(T):
                        act.wait_ge(scored, 8 * g + kt + 1)
                        if kt >= 4:
                            act.wait_ge(summed, 1 + 8 * g + kt - 3)
                        nc.scalar.activation(prob[:, kt % 4, :], banks[kt % 2][:, :], ACT.Exp, scale=SCALE_A).then_inc(exped, 1)

        @block.tensor
        def _(pe):
            for started in (transposed, summed,):
                pe.nop().then_inc(started, 1)
            pe.wait_ge(const_in, 48)
            pe.wait_ge(w_in, 16)
            with pe.Fori(0, B) as b:
                pe.wait_ge(recd, b * (HA + 1) + 1)
                for t in range(T):
                    last = nc.tensor.transpose(banks[0][:, t * P:(t + 1) * P], xn[:, t, :], ident[:, :])
                last.then_inc(transposed, 1)
                pe.wait_ge(xnt_ready, b + 1)
                for n in range(4):
                    for c in range(C):
                        nc.tensor.matmul(banks[(n + 1) % 4][:, c * CH:(c + 1) * CH], w[:, n * D:(n + 1) * D],
                                         xnt[:, c * CH:(c + 1) * CH], start=True, stop=True).then_inc(proj, 1)
                pe.wait_ge(rot, 4 * b + 4)
                for t in range(T):
                    last = nc.tensor.matmul(banks[0][:, t * P:(t + 1) * P], xnt[:, t * P:(t + 1) * P],
                                            w[:, 4 * D:5 * D], start=True, stop=True)
                last.then_inc(v_proj, 1)
                with pe.Fori(0, HA) as h:
                    g = b * HA + h
                    pe.wait_ge(zeroed, 5)
                    pe.wait_ge(v_ready, b + 1)
                    pe.wait_ge(stacks_in, NDMA_STACK * (b + 1))
                    for qt in range(T):
                        if qt >= 4:
                            pe.wait_ge(guard_max, 1 + 8 * g + qt - 3)
                        elif qt == 0:
                            pe.wait_ge(guard_max, 1 + 8 * g)
                        for c in range(C):
                            last = nc.tensor.matmul(banks[qt % 4][:, c * CH:(c + 1) * CH],
                                                    qs[0:SHIFT_ROW, bass.ds(h * S + qt * P, P)],
                                                    ks[0:SHIFT_ROW, bass.ds(h * S + c * CH, CH)], start=True, stop=True)
                        last.then_inc(guard, 1)
                pe.wait_ge(guard_max, 1 + 8 * HA * (b + 1))
                nc.tensor.transpose(banks[0][:, 0:P], negm[:, :], ident[:, :]).then_inc(m_trans, 1)
                with pe.Fori(0, HA // 2) as hh:
                    for par in range(2):
                        h = 2 * hh + par
                        g = b * HA + h
                        acc = banks[2 + par]

                        def score(kt):
                            if kt >= 2:
                                pe.wait_ge(exped, 8 * g + kt - 1)
                            elif kt == 0:
                                pe.wait_ge(m_in, 16 * b + 16)
                            for c in range(C):
                                last = nc.tensor.matmul(banks[kt % 2][:, c * CH:(c + 1) * CH],
                                                        ks[:, bass.ds(h * S + kt * P, P)],
                                                        qs[:, bass.ds(h * S + c * CH, CH)], start=True, stop=True)
                            last.then_inc(scored, 1)

                        def values(kt):
                            pe.wait_ge(masked, 8 * g + kt + 1)
                            if kt == 0:
                                pe.wait_ge(vh_ready, g + 1)
                                pe.wait_ge(normed[par], 1 + b * (HA // 2) + hh)
                            for c in range(C):
                                rows = acc[32 * c:32 * c + 32, :]
                                dc = kt - c * (CH // P)
                                if 0 <= dc < CH // P:
                                    nc.tensor.matmul(rows[:, dc * P:(dc + 1) * P], vh[:, kt, :], diag[:, kt % 2, :],
                                                     start=(kt == 0), stop=False, skip_group_check=True)
                                q0 = max(0, (dc + 1) * P)
                                if q0 < CH:
                                    nc.tensor.matmul(rows[:, q0:CH], vh[:, kt, :], prob[:, kt % 4, c * CH + q0:(c + 1) * CH],
                                                     start=(kt == 0 and c > 0), stop=False, skip_group_check=True)
                            for c in range(C):
                                last = nc.tensor.matmul(acc[64 + 32 * c:96 + 32 * c, 0:CH], ones[:, :],
                                                        prob[:, kt % 4, c * CH:(c + 1) * CH],
                                                        start=(kt == 0), stop=(kt == T - 1), skip_group_check=True)
                            last.then_inc(summed, 1)

                        score(0)
                        for kt in range(T):
                            if kt + 1 < T:
                                score(kt + 1)
                            values(kt)


def branch_b(nc, x, w_pair, w_oB, w_1, w_2, par_d, cB, cM, w_oA, xnt_scr, o_scr, out):
    with ExitStack() as ctx:
        sb = lambda n, s, d=F32: ctx.enter_context(nc.sbuf_tensor(n, s, d))
        ps = lambda n: ctx.enter_context(nc.psum_tensor(n, [P, S], F32))
        sem = lambda n: ctx.enter_context(nc.semaphore(n))
        base = sb("base", [P, 4, S])
        table = sb("table", [P, 4, S])
        consts = sb("consts", [P, CONSTS])
        ident, pairsum, mean_w = (consts[:, i * P:(i + 1) * P] for i in range(3))
        cmask = consts[:, 3 * P:3 * P + 3 * SPAN].rearrange("p (m n) -> p m n", m=3)
        mask = sb("mask", [P, 3, 2, SPAN], BF16)
        identb = sb("identb", [P, P], BF16)
        onesb = sb("onesb", [P, P], BF16)
        zerob = sb("zerob", [P, P], BF16)
        wo_a = sb("wo_a", [P, D])
        wqk, wv, wo = sb("wqk", [P, 4 * P]), sb("wv", [P, P]), sb("wo", [P, D])
        w1, w2 = sb("w1", [P, 2 * DIP]), sb("w2", [P, NJ, D])
        scales, par = sb("scales", [P, 4]), sb("par", [P, 9])
        xa, xb = sb("xa", [P, S + 1]), sb("xb", [P, S + 1])
        rcos, rsin, rsum = (sb(n, [P, 4, CH]) for n in ("rcos", "rsin", "rsum"))
        sq, ssq, lnss, rinv = (sb(n, [P, 4, CH]) for n in ("sq", "ssq", "lnss", "rinv"))
        qp = sb("qp", [P, 2, S + WIN])
        kk = sb("kk", [P, S])
        qpb = sb("qpb", [P, 2, S + WIN], BF16)
        kb = sb("kb", [P, WIN + S], BF16)
        negm = sb("negm", [P, T, 2])
        dm = sb("dm", [P, 2, S + WIN], BF16)
        va = sb("va", [P, T, 2, P])
        prob = sb("prob", [P, T, 2, SPAN])
        rec, ot = sb("rec", [P, CH]), sb("ot", [P, S])
        xcen, xsq, lnvar, rstd, xm, xnn = (t[:, 0:C, :].rearrange("p c n -> p (c n)")
                                           for t in (rcos, sq, lnss, rinv, rsin, rsum))
        gate, hid = sb("gate", [P, 2, CH]), sb("hid", [P, NJ, S])
        xtok, oa, yout = sb("xtok", [P, T, D]), sb("oa", [P, S]), sb("yout", [P, T, D])
        epsc = sb("epsc", [P, 2])
        pq, pS, po, py = (ps(n) for n in ("pq", "pS", "po", "py"))
        bank = lambda t, i: t[:, i * CH:(i + 1) * CH]

        const_in, base_in, woa_in = sem("const_in"), sem("base_in"), sem("woa_in")
        pool_init, dve_init = sem("pool_init"), sem("dve_init")
        wqk_in, wv_in, wo_in, ffw_in = sem("wqk_in"), sem("wv_in"), sem("wo_in"), sem("ffw_in")
        scales_in, xs_in, xtok_in, oa_in = sem("scales_in"), sem("xs_in"), sem("xtok_in"), sem("oa_in")
        table_ready = sem("table_ready")
        filled = sem("filled")
        dve_read, act_read = sem("dve_read"), sem("act_read")
        rot_sum = sem("rot_sum")
        ln_done, rinv_ready = sem("ln_done"), sem("rinv_ready")
        qk_ready = sem("qk_ready")
        bf_ready = sem("bf_ready")
        guard, negm_ready, diag_ready = sem("guard"), sem("negm_ready"), sem("diag_ready")
        scored, exped, valued = sem("scored"), sem("exped"), sem("valued")
        recd, o_ready, wo_done = sem("recd"), sem("o_ready"), sem("wo_done")
        xa_ready, xb_ready = sem("xa_ready"), sem("xb_ready")
        f_mean, f_cen, f_sq, f_var = sem("f_mean"), sem("f_cen"), sem("f_sq"), sem("f_var")
        f_ln, f_rstd, f_xm, f_xn = sem("f_ln"), sem("f_rstd"), sem("f_xm"), sem("f_xn")
        f_up, f_gate, f_hid, f_down = sem("f_up"), sem("f_gate"), sem("f_hid"), sem("f_down")
        straight, fin, fin_sum, out_saved = sem("straight"), sem("fin"), sem("fin_sum"), sem("out_saved")
        block = ctx.enter_context(nc.Block())
        proj_bank = lambda n: bank((pq, pS, po)[n % 6 // 2], n % 2)
        QK_BLOCKS = [(0, 0, 64), (1, 64, 128)]

        def units(eng, first, middle, last, before, after, batch_start, batch_end):
            with eng.Fori(0, B) as b:
                batch_start(b)
                with eng.Fori(0, L) as l:
                    f = b * L + l
                    before(b, l, f)
                    first(f, f * NP, l)
                    with eng.Fori(1, NP) as i:
                        middle(f, f * NP + i, l, i)
                    last(f, f * NP + NP, l)
                    after(b, l, f)
                batch_end(b)

        @block.sync
        def _(sp):
            for started in (out_saved,):
                sp.nop().then_inc(started, 1)
            sp.dma_start(consts[:, :], cM).then_inc(const_in, 16)
            sp.dma_start(base[:, :, :], cB).then_inc(base_in, 16)
            sp.dma_start(wo_a[:, :], w_oA).then_inc(woa_in, 16)

            with sp.Fori(0, B) as b:
                sp.wait_ge(fin, 1 + b)
                for lo, hi, off in ((0, 64, 0), (64, 128, 1)):
                    sp.dma_start(xa[lo:hi, off:off + S], xnt_scr[b, lo:hi, :]).then_inc(xs_in, 16)
                sp.dma_start(oa[:, :], o_scr[b]).then_inc(oa_in, 16)
                sp.wait_ge(fin_sum, 1 + b)
                sp.dma_start(xtok[:, :, :], x[b].rearrange("(t p) d -> p t d", p=P)).then_inc(xtok_in, 16)
                with sp.Fori(0, L) as l:
                    f = b * L + l
                    u = f * NP
                    sp.wait_ge(wo_done, 1 + u)
                    sp.dma_start(wqk[:, :], w_pair[l * NP, :, 0:4 * P]).then_inc(wqk_in, 16)
                    sp.dma_start(wv[:, :], w_pair[l * NP, :, 4 * P:5 * P]).then_inc(wv_in, 16)
                    sp.dma_start(wo[:, :], w_oB[l * NP]).then_inc(wo_in, 16)
                    sp.wait_ge(table_ready, 1 + 4 * f)
                    sp.dma_start(scales[:, :], par_d[l, :, 0:4]).then_inc(scales_in, 16)
                    sp.wait_ge(filled, 1 + ITEMS * u + 8)
                    sp.dma_start(wqk[:, :], w_pair[l * NP + 1, :, 0:4 * P]).then_inc(wqk_in, 16)
                    sp.wait_ge(xa_ready, 1 + f)
                    sp.dma_start(par[:, :], par_d[l, :, 4:13]).then_inc(ffw_in, 16)
                    sp.dma_start(w1[:, :], w_1[l]).then_inc(ffw_in, 16)
                    sp.dma_start(w2[:, :, :], w_2[l].rearrange("(j p) d -> p j d", p=P)).then_inc(ffw_in, 16)
                    with sp.Fori(1, NP - 1) as i:
                        sp.wait_ge(filled, 1 + ITEMS * (u + i - 1) + 10)
                        sp.dma_start(wv[:, :], w_pair[l * NP + i, :, 4 * P:5 * P]).then_inc(wv_in, 16)
                        sp.wait_ge(filled, 1 + ITEMS * (u + i) + 8)
                        sp.dma_start(wqk[:, :], w_pair[l * NP + i + 1, :, 0:4 * P]).then_inc(wqk_in, 16)
                        sp.wait_ge(wo_done, 1 + u + i)
                        sp.dma_start(wo[:, :], w_oB[l * NP + i]).then_inc(wo_in, 16)
                    sp.wait_ge(filled, 1 + ITEMS * (u + NP - 2) + 10)
                    sp.dma_start(wv[:, :], w_pair[l * NP + NP - 1, :, 4 * P:5 * P]).then_inc(wv_in, 16)
                    sp.wait_ge(wo_done, 1 + u + NP - 1)
                    sp.dma_start(wo[:, :], w_oB[l * NP + NP - 1]).then_inc(wo_in, 16)
                sp.wait_ge(fin_sum, 1 + b + 1)
                sp.dma_start(out[b].rearrange("(t p) d -> p t d", p=P), yout[:, :, :]).then_inc(out_saved, 16)
            sp.wait_ge(out_saved, 1 + 16 * B)

        @block.gpsimd
        def _(pool):
            for started in (qk_ready, rot_sum,):
                pool.nop().then_inc(started, 1)
            for t in (qp, qpb, dm):
                nc.gpsimd.memset(t[:, :, :], 0.0)
            nc.gpsimd.memset(kb[:, 0:WIN], 0.0)
            nc.gpsimd.memset(va[:, :, :, :], 1.0)
            nc.gpsimd.memset(onesb[:, :], 1.0)
            nc.gpsimd.memset(epsc[:, 0:1], EPS)
            nc.gpsimd.memset(epsc[:, 1:2], 12.0 * float(np.log(2.0)))
            nc.gpsimd.memset(zerob[:, :], 0.0).then_inc(pool_init, 1)
            pool.wait_ge(pool_init, 1)

            def add_rotated(u):
                for j in range(4):
                    pool.wait_ge(dve_read, 1 + ND * u + 2 * j + 2)
                    if j == 0:
                        pool.wait_ge(qk_ready, 1 + 6 * u)
                    nc.gpsimd.tensor_tensor(rsum[:, j, :], rcos[:, j, :], rsin[:, j, :], ALU.add).then_inc(rot_sum, 1)

            def diagonals(v):
                pool.wait_ge(negm_ready, T * v + T)
                pool.wait_ge(dve_init, 1)
                for h in range(2):
                    nc.gpsimd.tensor_tensor(dm[:, h, 0:S].rearrange("p (t n) -> p t n", t=T),
                                            identb[:, :].rearrange("p (o n) -> p o n", o=1).broadcast_to([P, T, P]),
                                            negm[:, :, h:h + 1].broadcast_to([P, T, P]), ALU.mult).then_inc(diag_ready, 1)

            def normalise(u, after_scores):
                for j in range(4):
                    pool.wait_ge(rinv_ready, 4 * u + j + 1)
                    if j == 0:
                        pool.wait_ge(rot_sum, 1 + 4 * u + 4)
                        if after_scores:
                            pool.wait_ge(scored, T * u)
                    c = j // 2
                    if j % 2 == 0:
                        for h, lo, hi in QK_BLOCKS:
                            pool.wait_ge(qk_ready, 1 + 6 * u + 3 * c + h)
                            nc.gpsimd.tensor_tensor(qp[lo:hi, h, c * CH:(c + 1) * CH], rsum[lo:hi, j, :],
                                                    rinv[lo:hi, j, :], ALU.mult).then_inc(qk_ready, 1)
                    else:
                        pool.wait_ge(qk_ready, 1 + 6 * u + 3 * c + 2)
                        nc.gpsimd.tensor_tensor(kk[:, c * CH:(c + 1) * CH], rsum[:, j, :], rinv[:, j, :],
                                                ALU.mult).then_inc(qk_ready, 1)

            def first(f, u, l):
                add_rotated(u)
                normalise(u, True)

            def middle(f, u, l, i):
                add_rotated(u)
                diagonals(u - 1)
                normalise(u, True)

            none = lambda b: None
            units(pool, first, middle, lambda f, u, l: diagonals(u - 1), lambda b, l, f: None, lambda b, l, f: None, none, none)

        @block.vector
        def _(dve):
            for started in (fin_sum, xa_ready, dve_read, o_ready,):
                dve.nop().then_inc(started, 1)
            dve.wait_ge(const_in, 16)
            nc.vector.memset(xa[64:128, 0:1], 0.0)
            nc.vector.memset(xb[64:128, 0:1], 0.0)
            nc.vector.tensor_copy(identb[:, :], ident)
            nc.vector.tensor_copy(mask[:, :, 0, :], cmask)
            nc.vector.tensor_copy(mask[:, :, 1, :], cmask).then_inc(dve_init, 1)

            def rotate(u, start):
                if start is not None:
                    dve.wait_ge(table_ready, 1 + 4 * start + 4)
                dve.wait_ge(rot_sum, 1 + 4 * u)
                for n in range(8):
                    dve.wait_ge(filled, 1 + ITEMS * u + n + 1)
                    c, k = n // 4, n % 4
                    dst = (rcos, rsin)[k % 2][:, 2 * c + k // 2, :]
                    nc.vector.tensor_tensor(dst, proj_bank(n), table[:, k, c * CH:(c + 1) * CH],
                                            ALU.mult).then_inc(dve_read, 1)

            def maxima(v):
                for qt in range(T):
                    dve.wait_ge(guard, T * v + qt + 1)
                    nc.vector.tensor_reduce(negm[:, qt, :], bank(pS, qt % 2)[:, 0:2 * SPAN].rearrange("p (h n) -> p h n", h=2),
                                            axis=AX.X, op=ALU.max, negate=True).then_inc(negm_ready, 1)

            def divide(v):
                for half, src in ((0, pq), (1, po)):
                    dve.wait_ge(valued, 2 * v + half + 1)
                    dve.wait_ge(o_ready, 1 + 2 * v + half)
                    nc.vector.reciprocal(rec[0:64, :], src[64:128, 0:CH])
                    nc.vector.reciprocal(rec[64:128, :], src[0:64, CH:2 * CH]).then_inc(recd, 1)
                    dve.wait_ge(recd, 2 * v + half + 1)
                    cols = slice(half * CH, (half + 1) * CH)
                    nc.vector.tensor_tensor(ot[0:64, cols], src[0:64, 0:CH], rec[0:64, :], ALU.mult)
                    nc.vector.tensor_tensor(ot[64:128, cols], src[64:128, CH:2 * CH], rec[64:128, :],
                                            ALU.mult).then_inc(o_ready, 1)

            def clamp(u):
                for j in range(4):
                    dve.wait_ge(filled, 1 + ITEMS * u + 10 + j + 1)
                    nc.vector.tensor_scalar(ssq[:, j, :], bank(pq, j % 2), 1e-24, None, ALU.max).then_inc(dve_read, 1)

            def first(f, u, l):
                rotate(u, f)
                clamp(u)

            def middle(f, u, l, i):
                rotate(u, None)
                maxima(u - 1)
                divide(u - 1)
                clamp(u)

            def last(f, u, l):
                maxima(u - 1)
                divide(u - 1)

            def after(b, l, f):
                dve.wait_ge(wo_done, 1 + NP * f + NP)
                for c in range(C):
                    for lo, hi, off in ((0, 64, 0), (64, 128, 1)):
                        cols = slice(c * CH + off, (c + 1) * CH + off)
                        ins = nc.vector.tensor_tensor(xb[lo:hi, cols], py[lo:hi, c * CH:(c + 1) * CH], xa[lo:hi, cols], ALU.add)
                ins.then_inc(xb_ready, 1)
                dve.wait_ge(xb_ready, f + 1)
                for c in range(C):
                    dve.wait_ge(f_mean, C * f + c + 1)
                    nc.vector.tensor_tensor(xcen[:, c * CH:(c + 1) * CH], xb[:, c * CH:(c + 1) * CH], bank(pq, c),
                                            ALU.subtract).then_inc(f_cen, 1)
                for c in range(C):
                    dve.wait_ge(f_rstd, C * f + c + 1)
                    if c == 0:
                        dve.wait_ge(f_cen, C * f + C)
                    nc.vector.tensor_tensor(xm[:, c * CH:(c + 1) * CH], xcen[:, c * CH:(c + 1) * CH],
                                            rstd[:, c * CH:(c + 1) * CH], ALU.mult).then_inc(f_xm, 1)
                for n in range(C * NJ):
                    c, j = n // NJ, n % NJ
                    dve.wait_ge(f_gate, C * NJ * f + n + 1)
                    nc.vector.scalar_tensor_tensor(hid[:, j, c * CH:(c + 1) * CH], (pq, pS)[n % 2][:, 0:CH],
                                                   par[:, 2 + j:3 + j], gate[:, n % 2, :], ALU.add, ALU.mult).then_inc(f_hid, 1)
                dve.wait_ge(f_down, C * f + C)
                for c in range(C):
                    for lo, hi, off in ((0, 64, 0), (64, 128, 1)):
                        cols = slice(c * CH + off, (c + 1) * CH + off)
                        ins = nc.vector.scalar_tensor_tensor(xa[lo:hi, cols], py[lo:hi, c * CH:(c + 1) * CH],
                                                             par[lo:hi, 8:9], xb[lo:hi, cols], ALU.add, ALU.add)
                ins.then_inc(xa_ready, 1)

            def batch_end(b):
                dve.wait_ge(xa_ready, 1 + L * b + L)
                for lo, hi, off in ((0, 64, 0), (64, 128, 1)):
                    ins = nc.vector.tensor_copy(ot[lo:hi, :], xa[lo:hi, off:off + S])
                ins.then_inc(straight, 1)
                dve.wait_ge(fin, 1 + b + 1)
                dve.wait_ge(xtok_in, 16 * b + 16)
                dve.wait_ge(out_saved, 1 + 16 * b)
                nc.vector.tensor_tensor(yout[:, :, :], pq[:, :].rearrange("p (t d) -> p t d", t=T), xtok[:, :, :],
                                        ALU.add).then_inc(fin_sum, 1)

            units(dve, first, middle, last, lambda b, l, f: None, after, lambda b: None, batch_end)

        @block.scalar
        def _(act):
            for started in (table_ready,):
                act.nop().then_inc(started, 1)
            act.wait_ge(pool_init, 1)

            def squares(u, js):
                for j in js:
                    n = (0, 2, 4, 6)[j]
                    act.wait_ge(dve_read, 1 + ND * u + n + 1)
                    nc.scalar.activation(sq[:, j, :], proj_bank(n), ACT.Square).then_inc(act_read, 1)

            def round_qk(v):
                act.wait_ge(qk_ready, 1 + 6 * v + 6)
                nc.scalar.activation(kb[:, WIN:WIN + S], kk[:, :], ACT.Copy).then_inc(bf_ready, 1)
                nc.scalar.activation(qpb[:, :, 0:S], qp[:, :, 0:S], ACT.Copy).then_inc(bf_ready, 1)

            def exps(v):
                for kt in range(T):
                    act.wait_ge(scored, T * v + kt + 1)
                    nc.scalar.activation(prob[:, kt, :, :], bank(pS, kt % 2)[:, 0:2 * SPAN].rearrange("p (h n) -> p h n", h=2),
                                         ACT.Exp).then_inc(exped, 1)

            def values_norms(u):
                for n in range(2):
                    act.wait_ge(filled, 1 + ITEMS * u + 8 + n + 1)
                    src = bank(pq, n).rearrange("p (t h d) -> p t h d", t=4, h=2)
                    for h in range(2):
                        ins = nc.scalar.activation(va[:, 4 * n:4 * n + 4, h, h * 64:h * 64 + 64], src[:, :, h, :], ACT.Copy)
                    ins.then_inc(act_read, 1)
                for j in range(4):
                    act.wait_ge(dve_read, 1 + ND * u + 8 + j + 1)
                    nc.scalar.activation(lnss[:, j, :], ssq[:, j, :], ACT.Ln, scale=2.0 ** 24).then_inc(ln_done, 1)
                for j in range(4):
                    act.wait_ge(ln_done, 4 * u + j + 1)
                    if j == 0:
                        act.wait_ge(qk_ready, 1 + 6 * u)
                    nc.scalar.activation(rinv[:, j, :], lnss[:, j, :], ACT.Exp, scale=-0.5,
                                         bias=epsc[:, 1:2]).then_inc(rinv_ready, 1)

            def first(f, u, l):
                squares(u, range(4))
                values_norms(u)

            def middle(f, u, l, i):
                squares(u, (0, 1))
                round_qk(u - 1)
                squares(u, (2, 3))
                exps(u - 1)
                values_norms(u)

            def last(f, u, l):
                round_qk(u - 1)
                exps(u - 1)

            def after(b, l, f):
                for c in range(C):
                    act.wait_ge(f_cen, C * f + c + 1)
                    nc.scalar.activation(xsq[:, c * CH:(c + 1) * CH], xcen[:, c * CH:(c + 1) * CH], ACT.Square).then_inc(f_sq, 1)
                for c in range(C):
                    act.wait_ge(f_var, C * f + c + 1)
                    nc.scalar.activation(lnvar[:, c * CH:(c + 1) * CH], bank(pS, c), ACT.Ln, bias=epsc[:, 0:1]).then_inc(f_ln, 1)
                for c in range(C):
                    act.wait_ge(f_ln, C * f + c + 1)
                    nc.scalar.activation(rstd[:, c * CH:(c + 1) * CH], lnvar[:, c * CH:(c + 1) * CH], ACT.Exp,
                                         scale=-0.5).then_inc(f_rstd, 1)
                for c in range(C):
                    act.wait_ge(f_xm, C * f + c + 1)
                    if c == 0:
                        act.wait_ge(ffw_in, 48 * f + 48)
                    nc.scalar.activation(xnn[:, c * CH:(c + 1) * CH], xm[:, c * CH:(c + 1) * CH], ACT.Identity,
                                         scale=par[:, 0:1], bias=par[:, 1:2]).then_inc(f_xn, 1)
                for n in range(C * NJ):
                    j = n % NJ
                    act.wait_ge(f_up, C * NJ * f + n + 1)
                    nc.scalar.activation(gate[:, n % 2, :], (pq, pS)[n % 2][:, CH:2 * CH], ACT.Gelu,
                                         bias=par[:, 5 + j:6 + j]).then_inc(f_gate, 1)

            def before(b, l, f):
                nc.scalar.preload_act_table_set(EXP_LN_SET)
                act.wait_ge(base_in, 16)
                act.wait_ge(scales_in, 16 * f + 16)
                act.wait_ge(dve_read, 1 + ND * NP * f)
                for k in range(4):
                    nc.scalar.activation(table[:, k, :], base[:, k, :], ACT.Copy, scale=scales[:, k:k + 1]).then_inc(table_ready, 1)

            units(act, first, middle, last, before, after, lambda b: None, lambda b: None)

        @block.tensor
        def _(pe):
            for started in (fin, filled, wo_done,):
                pe.nop().then_inc(started, 1)
            pe.wait_ge(pool_init, 1)
            pe.wait_ge(dve_init, 1)
            pe.wait_ge(const_in, 16)
            pe.wait_ge(woa_in, 16)

            def project_qk(u):
                pe.wait_ge(wqk_in, 16 * u + 16)
                pe.wait_ge(dve_read, 1 + ND * u)
                for n in range(8):
                    if n >= 6:
                        pe.wait_ge(dve_read, 1 + ND * u + upto(DVE_ITEMS, n - 6))
                        pe.wait_ge(act_read, NA * u + upto(ACT_ITEMS, n - 6))
                    c, k = n // 4, n % 4
                    nc.tensor.matmul(proj_bank(n), wqk[:, k * P:(k + 1) * P], xa[:, c * CH:(c + 1) * CH],
                                     start=True, stop=True).then_inc(filled, 1)

            def project_v_and_norms(u, pq_free):
                pe.wait_ge(wv_in, 16 * u + 16)
                pq_free()
                for n in range(2):
                    for t in range(4):
                        tt = 4 * n + t
                        last = nc.tensor.matmul(bank(pq, n)[:, t * P:(t + 1) * P], xa[:, tt * P:(tt + 1) * P], wv[:, :],
                                                start=True, stop=True)
                    last.then_inc(filled, 1)
                for j in range(4):
                    n = 10 + j
                    pe.wait_ge(act_read, NA * u + upto(ACT_ITEMS, n - 2))
                    pe.wait_ge(dve_read, 1 + ND * u + upto(DVE_ITEMS, n - 2))
                    nc.tensor.matmul(bank(pq, j % 2), pairsum, sq[:, j, :], start=True, stop=True).then_inc(filled, 1)

            def attend(v, pq_free):
                pe.wait_ge(bf_ready, 2 * v + 2)
                pq_free()
                for qt in range(T):
                    if qt >= 2:
                        pe.wait_ge(negm_ready, T * v + qt - 1)
                    dst = bank(pS, qt % 2)
                    for h in range(2):
                        nc.tensor.matmul(dst[:, h * SPAN:(h + 1) * SPAN], qpb[:, h, qt * P:(qt + 1) * P],
                                         kb[:, qt * P:qt * P + SPAN], start=(h == 0), stop=False, skip_group_check=True)
                    nc.tensor.matmul(dst[:, 0:2 * SPAN], identb[:, :], mask[:, 2 if qt == 0 else 1, :, :],
                                     start=False, stop=True, skip_group_check=True).then_inc(guard, 1)

                def score(kt):
                    if kt < 2:
                        pe.wait_ge(negm_ready, T * v + T - 1 + kt)
                    else:
                        pe.wait_ge(exped, T * v + kt - 1)
                    dst = bank(pS, kt % 2)[:, 0:2 * SPAN]
                    nc.tensor.matmul(dst, kk[:, kt * P:(kt + 1) * P], qp[:, :, kt * P:kt * P + SPAN],
                                     start=True, stop=False)
                    nc.tensor.matmul(dst, identb[:, :], mask[:, 0, :, :], start=False, stop=False)
                    if kt == 0:
                        pe.wait_ge(diag_ready, 2 * v + 2)
                    nc.tensor.matmul(dst, onesb[:, :], dm[:, :, kt * P:kt * P + SPAN], start=False,
                                     stop=True).then_inc(scored, 1)

                def values(kt):
                    pe.wait_ge(exped, T * v + kt + 1)
                    if kt == 0:
                        pe.wait_ge(act_read, NA * v + NA)
                    if kt == 3:
                        pe.wait_ge(o_ready, 1 + 2 * v)
                    for half, dst in ((0, pq), (1, po)):
                        lo, hi = max(kt * P, half * CH), min(kt * P + SPAN, (half + 1) * CH)
                        if lo >= hi:
                            continue
                        for h in range(2):
                            last = nc.tensor.matmul(bank(dst, h)[:, lo - half * CH:hi - half * CH], va[:, kt, h, :],
                                                    prob[:, kt, h, lo - kt * P:hi - kt * P],
                                                    start=(kt == (0, 3)[half]), stop=False, skip_group_check=True)
                        if (half, kt) in ((0, 3), (1, 7)):
                            last.then_inc(valued, 1)

                score(0)
                for kt in range(T):
                    if kt + 1 < T:
                        score(kt + 1)
                    values(kt)

            def project_out(v):
                pe.wait_ge(o_ready, 1 + 2 * v + 2)
                pe.wait_ge(wo_in, 16 * v + 16)
                for c in range(C):
                    last = nc.tensor.matmul(bank(py, c), wo[:, :], ot[:, c * CH:(c + 1) * CH], start=False, stop=False,
                                            skip_group_check=True)
                last.then_inc(wo_done, 1)

            def batch_start(b):
                pass

            def before(b, l, f):
                pe.wait_ge(xa_ready, 1 + f)
                pe.wait_ge(xs_in, 32 * b + 32)
                pe.wait_ge(fin_sum, 1 + b)
                for c in range(C):
                    nc.tensor.matmul(bank(py, c)[:, 0:2 * SPAN], zerob[:, :], mask[:, 0, :, :], start=True, stop=False,
                                     skip_group_check=True)
                    nc.tensor.matmul(bank(py, c)[:, 2 * SPAN:CH], zerob[:, :], dm[:, 0, 0:CH - 2 * SPAN], start=False,
                                     stop=False, skip_group_check=True)

            def first(f, u, l):
                project_qk(u)
                project_v_and_norms(u, lambda: (pe.wait_ge(dve_read, 1 + ND * u + 8), pe.wait_ge(act_read, NA * u + 4)))

            def middle(f, u, l, i):
                v = u - 1
                project_qk(u)
                attend(v, lambda: (pe.wait_ge(dve_read, 1 + ND * u + 8), pe.wait_ge(act_read, NA * u + 4)))
                project_v_and_norms(u, lambda: pe.wait_ge(o_ready, 1 + 2 * v + 1))
                project_out(v)

            def last(f, u, l):
                attend(u - 1, lambda: pe.wait_ge(dve_read, 1 + ND * u))
                project_out(u - 1)

            def after(b, l, f):
                pe.wait_ge(xb_ready, f + 1)
                for c in range(C):
                    nc.tensor.matmul(bank(pq, c), mean_w, xb[:, c * CH:(c + 1) * CH], start=True, stop=True).then_inc(f_mean, 1)
                for c in range(C):
                    pe.wait_ge(f_sq, C * f + c + 1)
                    nc.tensor.matmul(bank(pS, c), mean_w, xsq[:, c * CH:(c + 1) * CH], start=True, stop=True).then_inc(f_var, 1)
                pe.wait_ge(f_xn, C * f + C)
                pe.wait_ge(ffw_in, 48 * f + 48)
                for n in range(C * NJ):
                    c, j = n // NJ, n % NJ
                    if n >= 2:
                        pe.wait_ge(f_hid, C * NJ * f + n - 1)
                    for k in range(2):
                        last = nc.tensor.matmul((pq, pS)[n % 2][:, k * CH:(k + 1) * CH],
                                                w1[:, k * DIP + j * P:k * DIP + (j + 1) * P],
                                                xnn[:, c * CH:(c + 1) * CH], start=True, stop=True)
                    last.then_inc(f_up, 1)
                for c in range(C):
                    pe.wait_ge(f_hid, C * NJ * f + (c + 1) * NJ)
                    for j in range(NJ):
                        last = nc.tensor.matmul(bank(py, c), w2[:, j, :], hid[:, j, c * CH:(c + 1) * CH],
                                                start=(j == 0), stop=(j == NJ - 1))
                    last.then_inc(f_down, 1)

            def batch_end(b):
                pe.wait_ge(straight, b + 1)
                pe.wait_ge(oa_in, 16 * b + 16)
                for t in range(T):
                    dst = pq[:, t * P:(t + 1) * P]
                    nc.tensor.matmul(dst, oa[:, t * P:(t + 1) * P], wo_a[:, :], start=(t % 4 == 0), stop=False,
                                     skip_group_check=True)
                    last = nc.tensor.matmul(dst, ot[:, t * P:(t + 1) * P], ident, start=False, stop=False,
                                            skip_group_check=True)
                last.then_inc(fin, 1)

            units(pe, first, middle, last, before, after, batch_start, batch_end)


def build(nc, a, out):
    o_scr = nc.dram_tensor("o_scr", (B, D, S), F32).ap()
    xnt_scr = nc.dram_tensor("xnt_scr", (B, D, S), F32).ap()
    part_scr = nc.dram_tensor("part_scr", (2, 3, D, S), BF16).ap()
    m_scr = nc.dram_tensor("m_scr", (P, P), BF16).ap()
    branch_a(nc, a["x"], a["wA"], a["cA"], a["cM"][:, 0:P], a["cM"][:, CONSTS - P:CONSTS], o_scr, xnt_scr, part_scr, m_scr)
    branch_b(nc, a["x"], a["w_pair"], a["w_oB"], a["w_1"], a["w_2"], a["par"], a["cB"], a["cM"], a["w_oA"],
             xnt_scr, o_scr, out)


def position_constants():
    f = np.float32
    t = np.arange(S, dtype=f)
    inv = f(10000.0) ** (-(np.arange(DA // 2, dtype=f) * f(2.0) / f(DA)))
    ang = (t[:, None] * inv[None, :]).astype(f)
    d = np.arange(DA)
    sign = np.where(d % 2 == 0, f(-1), f(1))
    cA = np.stack([np.tile(np.cos(ang)[:, d // 2].T, (HA, 1)),
                   np.tile((np.sin(ang)[:, d // 2] * sign).T, (HA, 1))], 1).astype(f)
    half = np.arange(0, DB, 2, dtype=f)
    inv = (f(1.0) / f(10000.0) ** (half / f(DB))).astype(f)
    fr = (t[:, None] * inv[None, :]).astype(f)
    base = ((half + f(0.4 * DB)) / f(1.4 * DB)).astype(f)
    power = ((t - f(S // 2)) / f(WIN // 2)).astype(f)
    sc = (base[None, :] ** power[:, None]).astype(f)
    fr, sc = np.concatenate([fr, fr], -1), np.concatenate([sc, sc], -1)
    sign = np.where(np.arange(DB) < DB // 2, f(-1), f(1))[None, :]
    isc = (f(1.0) / sc).astype(f)
    tabs = [np.cos(fr) * sc * f(8), np.sin(fr) * sc * sign * f(8), np.cos(fr) * isc, np.sin(fr) * isc * sign]
    cB = np.stack([np.tile(x.T, (2, 1)) for x in tabs], 1).astype(f)
    p, n = np.arange(P)[:, None], np.arange(SPAN)[None, :]
    off = f(-1e30)
    by_key = np.where((n >= p) & (n <= p + WIN), f(0), off)
    by_query = by_key
    first = np.where(n < WIN, off, by_query)
    pair = (np.arange(P)[:, None] // DB == np.arange(P)[None, :] // DB).astype(f)
    cM = np.concatenate([np.eye(P, dtype=f), pair, np.full((P, P), f(1.0 / D)), by_key, by_query, first,
                         np.triu(np.ones((P, P), f))], 1).astype(f)
    return np.ascontiguousarray(cA), np.ascontiguousarray(cB), np.ascontiguousarray(cM)


def lay_out(i):
    c = np.ascontiguousarray
    swap = np.arange(D) ^ 1
    wq, wk, wv = (np.asarray(i[f"L0_attn_w_{n}"]).T for n in "qkv")
    wA = c(np.concatenate([wq, wq[:, swap], wk, wk[:, swap], wv], 1))
    W = np.asarray(i["L0_ffn_Wqkv"]).reshape(L, D, 3, NP, 2, DB)
    rot = np.concatenate([np.arange(DB // 2, DB), np.arange(DB // 2)])
    q, k, v = (W[:, :, n].transpose(0, 2, 1, 3, 4) for n in range(3))
    w_pair = c(np.stack([q, q[..., rot], k, k[..., rot], v], 3).reshape(L * NP, D, 5 * P))
    w_oB = c(np.asarray(i["L0_ffn_Wo"]).reshape(L * NP, P, D))
    pad = ((0, 0), (0, 0), (0, DIP - DI))
    W1 = np.asarray(i["L0_ffn_W1"])
    w_1 = c(np.concatenate([np.pad(W1[:, :, :DI], pad), np.pad(W1[:, :, DI:], pad)], 2))
    w_2 = c(np.pad(np.asarray(i["L0_ffn_W2"]), ((0, 0), (0, DIP - DI), (0, 0))))
    qs, ks = np.asarray(i["L0_ffn_q_scale"]), np.asarray(i["L0_ffn_k_scale"])
    two = lambda s: np.concatenate([s, s], 1)[:, :, None]
    b1 = np.asarray(i["L0_ffn_b1"])
    cols = lambda s: np.pad(s, ((0, 0), (0, DIP - DI))).reshape(L, NJ, P).transpose(0, 2, 1)
    par = c(np.concatenate([two(qs), two(qs[:, rot]), two(ks), two(ks[:, rot]),
                            np.asarray(i["L0_ffn_ln_g"])[:, :, None], np.asarray(i["L0_ffn_ln_b"])[:, :, None],
                            cols(b1[:, :DI]), cols(b1[:, DI:]), np.asarray(i["L0_ffn_b2"])[:, :, None]], 2))
    cA, cB, cM = position_constants()
    return {"x": c(np.asarray(i["L0_attn_x"])), "wA": wA, "w_oA": c(np.asarray(i["L0_attn_w_o"]).T), "w_pair": w_pair,
            "w_oB": w_oB, "w_1": w_1, "w_2": w_2, "par": par, "cA": cA, "cB": cB, "cM": cM}


def kernel(**inputs):
    import concourse.bacc as bacc
    from concourse.bass_utils import run_bass_kernel_spmd

    nc = bacc.Bacc("TRN2", target_bir_lowering=False, num_devices=1)
    arrays = lay_out(inputs)
    aps = {n: nc.dram_tensor(f"in_{n}", v.shape, mybir.dt.from_np(v.dtype), kind="ExternalInput").ap()
           for n, v in arrays.items()}
    out = nc.dram_tensor("out", (B, S, D), F32, kind="ExternalOutput").ap()
    build(nc, aps, out)
    r = run_bass_kernel_spmd(nc, [{f"in_{n}": v for n, v in arrays.items()}], core_ids=[0])
    return r.results[0]["out"]
```

```python
import numpy as np
import concourse.bass as bass
from concourse import mybir
from contextlib import ExitStack

F32 = mybir.dt.float32
BF16 = mybir.dt.bfloat16
ACT = mybir.ActivationFunctionType
ALU = mybir.AluOpType
AX = mybir.AxisListType

B, S, D = 4, 1024, 128
P = 128
T = S // P
CH = 512
C = S // CH
HA, DA = 16, 8
SCALE_A = 1.0 / float(np.sqrt(DA))
TERMS_Q = [0, 0, 1, 1, 0, 2]
TERMS_K = [0, 1, 0, 1, 2, 0]
SHIFT_ROW = 96
EPS = 1e-5
L, HB, DB, WIN = 6, 16, 64, 32
NP = HB // 2
SPAN = P + WIN
DI = 341
NJ = 3
DIP = NJ * P
HALF = DB
EXP_LN_SET = "natural_log_exp_and_others"
CONSTS = 4 * P + 3 * SPAN
ITEMS = 14
DVE_ITEMS = (0, 1, 2, 3, 4, 5, 6, 7, 8, 9, 10, 11)
ACT_ITEMS = (0, 2, 4, 6, 12, 13)
ND, NA = len(DVE_ITEMS), len(ACT_ITEMS)


def upto(items, n):
    return sum(i <= n for i in items)


def branch_a(nc, x, wA, cA, ident_d, causal_d, o_scr, xnt_scr, part_scr, m_scr):
    with ExitStack() as ctx:
        sb = lambda n, s, d=F32: ctx.enter_context(nc.sbuf_tensor(n, s, d))
        ps = lambda n: ctx.enter_context(nc.psum_tensor(n, [P, S], F32))
        sem = lambda n: ctx.enter_context(nc.semaphore(n))
        ident = sb("a_ident", [P, P])
        w = sb("a_w", [P, 5 * D])
        causal = sb("a_causal", [P, P])
        rope = sb("a_rope", [P, 2, S])
        xtok = sb("a_xtok", [P, T, D])
        xc = sb("a_xc", [P, T, D])
        sq = sb("a_sq", [P, T, D])
        mean, var, rstd = sb("a_mean", [P, T]), sb("a_var", [P, T]), sb("a_rstd", [P, T])
        std = sb("a_std", [P, T])
        xn = sb("a_xn", [P, T, D])
        xnt = sb("a_xnt", [P, S])
        cosq = sb("a_cosq", [P, 2, S])
        sinq = sb("a_sinq", [P, 2, S])
        rest = sb("a_rest", [P, 2, S])
        parts = sb("a_parts", [P, 2, 3, S], BF16)
        v = sb("a_v", [P, T, D])
        qs = sb("a_qstack", [P, HA * S], BF16)
        ks = sb("a_kstack", [P, HA * S], BF16)
        negm = sb("a_negm", [P, HA * T])
        negmt = sb("a_negmt", [P, P], BF16)
        vh = sb("a_vh", [P, T, 32])
        ones = sb("a_ones", [P, 32])
        prob = sb("a_prob", [P, 4, S])
        diag = sb("a_diag", [P, 2, P])
        rec = sb("a_rec", [64, 2, CH])
        oh = sb("a_oh", [64, 2, CH])
        banks = [ps(f"a_ps{i}") for i in range(4)]

        const_in, w_in = sem("a_const_in"), sem("a_w_in")
        x_in, xnt_saved = sem("a_x_in"), sem("a_xnt_saved")
        zeroed = sem("a_zeroed")
        ln = sem("a_ln")
        std_done = sem("a_std_done")
        transposed, xnt_ready = sem("a_transposed"), sem("a_xnt_ready")
        proj, rot = sem("a_proj"), sem("a_rot")
        v_proj, v_ready = sem("a_v_proj"), sem("a_v_ready")
        rotated = sem("a_rotated")
        split = sem("a_split")
        parts_out, stacks_in = sem("a_parts_out"), sem("a_stacks_in")
        guard, guard_max = sem("a_guard"), sem("a_guard_max")
        m_trans, m_ready = sem("a_m_trans"), sem("a_m_ready")
        m_out, m_in = sem("a_m_out"), sem("a_m_in")
        scored, exped, masked, summed = sem("a_scored"), sem("a_exped"), sem("a_masked"), sem("a_summed")
        vh_ready, recd = sem("a_vh_ready"), sem("a_recd")
        normed = [sem("a_normed0"), sem("a_normed1")]
        o_saved = [sem("a_o_saved0"), sem("a_o_saved1")]
        block = ctx.enter_context(nc.Block())
        NDMA_STACK = 16 * 2 * len(TERMS_Q)

        @block.sync
        def _(sp):
            for started in (xnt_saved, parts_out, m_out, o_saved[0], o_saved[1],):
                sp.nop().then_inc(started, 1)
            sp.dma_start(ident[:, :], ident_d).then_inc(const_in, 16)
            sp.dma_start(causal[:, :], causal_d).then_inc(const_in, 16)
            sp.dma_start(rope[:, :, :], cA).then_inc(const_in, 16)
            sp.dma_start(w[:, :], wA).then_inc(w_in, 16)
            with sp.Fori(0, B) as b:
                sp.wait_ge(ln, 1 + 7 * b)
                sp.dma_start(xtok[:, :, :], x[b].rearrange("(t p) d -> p t d", p=P)).then_inc(x_in, 16)
                sp.wait_ge(xnt_ready, b + 1)
                sp.dma_start(xnt_scr[b], xnt[:, :]).then_inc(xnt_saved, 16)
                for side in range(2):
                    sp.wait_ge(split, 6 * b + 5 + side)
                    sp.dma_start(part_scr[side].rearrange("t p n -> p t n"), parts[:, side, :, :]).then_inc(parts_out, 16)
                sp.wait_ge(parts_out, 1 + 32 * b + 32)
                sp.wait_ge(zeroed, 5)
                for stack, side, terms in ((qs, 0, TERMS_Q), (ks, 1, TERMS_K)):
                    for t, part in enumerate(terms):
                        sp.dma_start(stack[DA * t:DA * t + DA, :].rearrange("r (h n) -> r h n", h=HA),
                                     part_scr[side, part].rearrange("(h r) n -> r h n", r=DA)).then_inc(stacks_in, 16)
                sp.wait_ge(m_ready, b + 1)
                sp.dma_start(m_scr, negmt[:, :]).then_inc(m_out, 16)
                sp.wait_ge(m_out, 1 + 16 * b + 16)
                sp.dma_start(qs[SHIFT_ROW:SHIFT_ROW + 1, :], m_scr.rearrange("(a m) n -> a (m n)", a=1)).then_inc(m_in, 16)
                with sp.Fori(0, HA // 2) as hh:
                    for par in range(2):
                        g = b * (HA // 2) + hh
                        sp.wait_ge(normed[par], 1 + g + 1)
                        for c in range(C):
                            sp.dma_start(o_scr[b, bass.ds((2 * hh + par) * DA, DA), c * CH:(c + 1) * CH],
                                         oh[32 * c:32 * c + DA, par, :]).then_inc(o_saved[par], 16)
            sp.wait_ge(xnt_saved, 1 + 16 * B)
            for par in range(2):
                sp.wait_ge(o_saved[par], 1 + 32 * B * HA // 2)

        @block.gpsimd
        def _(pool):
            nc.gpsimd.memset(qs[:, :], 0.0).then_inc(zeroed, 1)
            nc.gpsimd.memset(ks[:, :], 0.0).then_inc(zeroed, 1)
            nc.gpsimd.memset(vh[:, :, :], 0.0).then_inc(zeroed, 1)
            nc.gpsimd.memset(ones[:, :], 1.0).then_inc(zeroed, 1)
            pool.wait_ge(zeroed, 4)
            pool.wait_ge(const_in, 48)
            nc.gpsimd.memset(ks[SHIFT_ROW:SHIFT_ROW + 1, :], 1.0).then_inc(zeroed, 1)
            pool.wait_ge(zeroed, 5)
            with pool.Fori(0, B) as b:
                for side in range(2):
                    pool.wait_ge(rot, 4 * b + 2 * side + 2)
                    nc.gpsimd.tensor_tensor(rest[:, side, :], cosq[:, side, :], sinq[:, side, :], ALU.add).then_inc(rotated, 1)
                for step in range(2):
                    for side in range(2):
                        pool.wait_ge(split, 6 * b + 2 * step + side + 1)
                        pool.wait_ge(rotated, 6 * b + 2 * step + side + 1)
                        nc.gpsimd.tensor_tensor(rest[:, side, :], rest[:, side, :], parts[:, side, step, :],
                                                ALU.subtract).then_inc(rotated, 1)
                with pool.Fori(0, HA) as h:
                    g = b * HA + h
                    pool.wait_ge(v_ready, b + 1)
                    pool.wait_ge(summed, 1 + 8 * g)
                    nc.gpsimd.tensor_copy(vh[:, :, 0:DA], v[:, :, bass.ds(h * DA, DA)]).then_inc(vh_ready, 1)
                    for kt in range(T):
                        pool.wait_ge(exped, 8 * g + kt + 1)
                        if kt >= 2:
                            pool.wait_ge(summed, 1 + 8 * g + kt - 1)
                        nc.gpsimd.tensor_tensor(diag[:, kt % 2, :], prob[:, kt % 4, kt * P:(kt + 1) * P], causal[:, :],
                                                ALU.mult).then_inc(masked, 1)

        @block.vector
        def _(dve):
            for started in (ln, guard_max, normed[0], normed[1],):
                dve.nop().then_inc(started, 1)
            with dve.Fori(0, B) as b:
                dve.wait_ge(x_in, 16 * b + 16)
                dve.wait_ge(transposed, 1 + b)
                n = 7 * b
                bc = lambda t: t[:, :].rearrange("p (t o) -> p t o", o=1).broadcast_to([P, T, D])
                nc.vector.tensor_reduce(mean[:, :], xtok[:, :, :], axis=AX.X, op=ALU.add).then_inc(ln, 1)
                dve.wait_ge(ln, 1 + n + 1)
                nc.vector.tensor_scalar(mean[:, :], mean[:, :], 1.0 / D, None, ALU.mult).then_inc(ln, 1)
                dve.wait_ge(ln, 1 + n + 2)
                nc.vector.tensor_tensor(xc[:, :, :], xtok[:, :, :], bc(mean), ALU.subtract).then_inc(ln, 1)
                dve.wait_ge(ln, 1 + n + 3)
                nc.vector.tensor_tensor(sq[:, :, :], xc[:, :, :], xc[:, :, :], ALU.mult).then_inc(ln, 1)
                dve.wait_ge(ln, 1 + n + 4)
                nc.vector.tensor_reduce(var[:, :], sq[:, :, :], axis=AX.X, op=ALU.add).then_inc(ln, 1)
                dve.wait_ge(ln, 1 + n + 5)
                nc.vector.tensor_scalar(var[:, :], var[:, :], 1.0 / D, EPS, ALU.mult, ALU.add).then_inc(ln, 1)
                dve.wait_ge(std_done, b + 1)
                nc.vector.reciprocal(rstd[:, :], std[:, :]).then_inc(ln, 1)
                dve.wait_ge(ln, 1 + n + 7)
                nc.vector.tensor_tensor(xn[:, :, :], xc[:, :, :], bc(rstd), ALU.mult).then_inc(recd, 1)
                dve.wait_ge(transposed, 1 + b + 1)
                dve.wait_ge(xnt_saved, 1 + 16 * b)
                nc.vector.tensor_copy(xnt[:, :], banks[0][:, :]).then_inc(xnt_ready, 1)
                dve.wait_ge(const_in, 48)
                for side in range(2):
                    for k, dst in ((0, cosq), (1, sinq)):
                        n4 = 2 * side + k
                        dve.wait_ge(proj, 8 * b + 2 * n4 + 2)
                        nc.vector.tensor_tensor(dst[:, side, :], banks[(n4 + 1) % 4][:, :], rope[:, k, :],
                                                ALU.mult).then_inc(rot, 1)
                with dve.Fori(0, HA) as h:
                    g = b * HA + h
                    for qt in range(T):
                        dve.wait_ge(guard, 8 * g + qt + 1)
                        nc.vector.tensor_reduce(negm[:, bass.ds(h * T + qt, 1)], banks[qt % 4][:, :], axis=AX.X,
                                                op=ALU.max, negate=True).then_inc(guard_max, 1)
                dve.wait_ge(m_trans, b + 1)
                dve.wait_ge(m_out, 1 + 16 * b)
                nc.vector.tensor_copy(negmt[:, :], banks[0][:, 0:P]).then_inc(m_ready, 1)
                with dve.Fori(0, HA // 2) as hh:
                    g = b * (HA // 2) + hh
                    for par in range(2):
                        acc = banks[2 + par]
                        dve.wait_ge(summed, 1 + 8 * (2 * g + par) + 8)
                        dve.wait_ge(normed[par], 1 + g)
                        nc.vector.reciprocal(rec[:, par, :], acc[64:128, 0:CH]).then_inc(recd, 1)
                        dve.wait_ge(recd, b + 2 * g + par + 2)
                        dve.wait_ge(o_saved[par], 1 + 32 * g)
                        nc.vector.tensor_tensor(oh[:, par, :], acc[0:64, 0:CH], rec[:, par, :], ALU.mult).then_inc(normed[par], 1)

        @block.scalar
        def _(act):
            with act.Fori(0, B) as b:
                act.wait_ge(ln, 1 + 7 * b + 6)
                nc.scalar.activation(std[:, :], var[:, :], ACT.Sqrt).then_inc(std_done, 1)
                nc.scalar.preload_act_table_set("exp_and_others")
                for part in range(3):
                    for side in range(2):
                        if part == 0:
                            act.wait_ge(parts_out, 1 + 32 * b)
                        act.wait_ge(rotated, 6 * b + 2 * part + side + 1)
                        nc.scalar.activation(parts[:, side, part, :], rest[:, side, :], ACT.Copy).then_inc(split, 1)
                act.wait_ge(v_proj, b + 1)
                nc.scalar.activation(v[:, :, :], banks[0][:, :].rearrange("p (t d) -> p t d", t=T), ACT.Copy).then_inc(v_ready, 1)
                with act.Fori(0, HA) as h:
                    g = b * HA + h
                    for kt in range(T):
                        act.wait_ge(scored, 8 * g + kt + 1)
                        if kt >= 4:
                            act.wait_ge(summed, 1 + 8 * g + kt - 3)
                        nc.scalar.activation(prob[:, kt % 4, :], banks[kt % 2][:, :], ACT.Exp, scale=SCALE_A).then_inc(exped, 1)

        @block.tensor
        def _(pe):
            for started in (transposed, summed,):
                pe.nop().then_inc(started, 1)
            pe.wait_ge(const_in, 48)
            pe.wait_ge(w_in, 16)
            with pe.Fori(0, B) as b:
                pe.wait_ge(recd, b * (HA + 1) + 1)
                for t in range(T):
                    last = nc.tensor.transpose(banks[0][:, t * P:(t + 1) * P], xn[:, t, :], ident[:, :])
                last.then_inc(transposed, 1)
                pe.wait_ge(xnt_ready, b + 1)
                for n in range(4):
                    for c in range(C):
                        nc.tensor.matmul(banks[(n + 1) % 4][:, c * CH:(c + 1) * CH], w[:, n * D:(n + 1) * D],
                                         xnt[:, c * CH:(c + 1) * CH], start=True, stop=True).then_inc(proj, 1)
                pe.wait_ge(rot, 4 * b + 4)
                for t in range(T):
                    last = nc.tensor.matmul(banks[0][:, t * P:(t + 1) * P], xnt[:, t * P:(t + 1) * P],
                                            w[:, 4 * D:5 * D], start=True, stop=True)
                last.then_inc(v_proj, 1)
                with pe.Fori(0, HA) as h:
                    g = b * HA + h
                    pe.wait_ge(zeroed, 5)
                    pe.wait_ge(v_ready, b + 1)
                    pe.wait_ge(stacks_in, NDMA_STACK * (b + 1))
                    for qt in range(T):
                        if qt >= 4:
                            pe.wait_ge(guard_max, 1 + 8 * g + qt - 3)
                        elif qt == 0:
                            pe.wait_ge(guard_max, 1 + 8 * g)
                        for c in range(C):
                            last = nc.tensor.matmul(banks[qt % 4][:, c * CH:(c + 1) * CH],
                                                    qs[0:SHIFT_ROW, bass.ds(h * S + qt * P, P)],
                                                    ks[0:SHIFT_ROW, bass.ds(h * S + c * CH, CH)], start=True, stop=True)
                        last.then_inc(guard, 1)
                pe.wait_ge(guard_max, 1 + 8 * HA * (b + 1))
                nc.tensor.transpose(banks[0][:, 0:P], negm[:, :], ident[:, :]).then_inc(m_trans, 1)
                with pe.Fori(0, HA // 2) as hh:
                    for par in range(2):
                        h = 2 * hh + par
                        g = b * HA + h
                        acc = banks[2 + par]

                        def score(kt):
                            if kt >= 2:
                                pe.wait_ge(exped, 8 * g + kt - 1)
                            elif kt == 0:
                                pe.wait_ge(m_in, 16 * b + 16)
                            for c in range(C):
                                last = nc.tensor.matmul(banks[kt % 2][:, c * CH:(c + 1) * CH],
                                                        ks[:, bass.ds(h * S + kt * P, P)],
                                                        qs[:, bass.ds(h * S + c * CH, CH)], start=True, stop=True)
                            last.then_inc(scored, 1)

                        def values(kt):
                            pe.wait_ge(masked, 8 * g + kt + 1)
                            if kt == 0:
                                pe.wait_ge(vh_ready, g + 1)
                                pe.wait_ge(normed[par], 1 + b * (HA // 2) + hh)
                            for c in range(C):
                                rows = acc[32 * c:32 * c + 32, :]
                                dc = kt - c * (CH // P)
                                if 0 <= dc < CH // P:
                                    nc.tensor.matmul(rows[:, dc * P:(dc + 1) * P], vh[:, kt, :], diag[:, kt % 2, :],
                                                     start=(kt == 0), stop=False, skip_group_check=True)
                                q0 = max(0, (dc + 1) * P)
                                if q0 < CH:
                                    nc.tensor.matmul(rows[:, q0:CH], vh[:, kt, :], prob[:, kt % 4, c * CH + q0:(c + 1) * CH],
                                                     start=(kt == 0 and c > 0), stop=False, skip_group_check=True)
                            for c in range(C):
                                last = nc.tensor.matmul(acc[64 + 32 * c:96 + 32 * c, 0:CH], ones[:, :],
                                                        prob[:, kt % 4, c * CH:(c + 1) * CH],
                                                        start=(kt == 0), stop=(kt == T - 1), skip_group_check=True)
                            last.then_inc(summed, 1)

                        score(0)
                        for kt in range(T):
                            if kt + 1 < T:
                                score(kt + 1)
                            values(kt)


def branch_b(nc, x, w_pair, w_oB, w_1, w_2, par_d, cB, cM, w_oA, xnt_scr, o_scr, out):
    with ExitStack() as ctx:
        sb = lambda n, s, d=F32: ctx.enter_context(nc.sbuf_tensor(n, s, d))
        ps = lambda n: ctx.enter_context(nc.psum_tensor(n, [P, S], F32))
        sem = lambda n: ctx.enter_context(nc.semaphore(n))
        base = sb("base", [P, 4, S])
        table = sb("table", [P, 4, S])
        consts = sb("consts", [P, CONSTS])
        ident, pairsum, mean_w = (consts[:, i * P:(i + 1) * P] for i in range(3))
        cmask = consts[:, 3 * P:3 * P + 3 * SPAN].rearrange("p (m n) -> p m n", m=3)
        mask = sb("mask", [P, 3, 2, SPAN], BF16)
        identb = sb("identb", [P, P], BF16)
        onesb = sb("onesb", [P, P], BF16)
        zerob = sb("zerob", [P, P], BF16)
        wo_a = sb("wo_a", [P, D])
        wqk, wv, wo = sb("wqk", [P, 4 * P]), sb("wv", [P, P]), sb("wo", [P, D])
        w1, w2 = sb("w1", [P, 2 * DIP]), sb("w2", [P, NJ, D])
        scales, par = sb("scales", [P, 4]), sb("par", [P, 9])
        xa, xb = sb("xa", [P, S + 1]), sb("xb", [P, S + 1])
        rcos, rsin, rsum = (sb(n, [P, 4, CH]) for n in ("rcos", "rsin", "rsum"))
        sq, ssq, lnss, rinv = (sb(n, [P, 4, CH]) for n in ("sq", "ssq", "lnss", "rinv"))
        qp = sb("qp", [P, 2, S + WIN])
        kk = sb("kk", [P, S])
        qpb = sb("qpb", [P, 2, S + WIN], BF16)
        kb = sb("kb", [P, WIN + S], BF16)
        negm = sb("negm", [P, T, 2])
        dm = sb("dm", [P, 2, S + WIN], BF16)
        va = sb("va", [P, T, 2, P])
        prob = sb("prob", [P, T, 2, SPAN])
        rec, lnden, ot = sb("rec", [P, 2, CH]), sb("lnden", [P, 2, CH]), sb("ot", [P, S])
        xcen, xsq, lnvar, rstd, xm, xnn = (t[:, 0:C, :].rearrange("p c n -> p (c n)")
                                           for t in (rcos, sq, lnss, rinv, rsin, rsum))
        gate, hid = sb("gate", [P, 2, CH]), sb("hid", [P, NJ, S])
        xtok, oa, yout = sb("xtok", [P, T, D]), sb("oa", [P, S]), sb("yout", [P, T, D])
        epsc = sb("epsc", [P, 2])
        pq, pS, po, py = (ps(n) for n in ("pq", "pS", "po", "py"))
        bank = lambda t, i: t[:, i * CH:(i + 1) * CH]

        const_in, base_in, woa_in = sem("const_in"), sem("base_in"), sem("woa_in")
        pool_init, dve_init = sem("pool_init"), sem("dve_init")
        wqk_in, wv_in, wo_in, ffw_in = sem("wqk_in"), sem("wv_in"), sem("wo_in"), sem("ffw_in")
        scales_in, xs_in, xtok_in, oa_in = sem("scales_in"), sem("xs_in"), sem("xtok_in"), sem("oa_in")
        table_ready = sem("table_ready")
        filled = sem("filled")
        dve_read, act_read = sem("dve_read"), sem("act_read")
        rot_sum = sem("rot_sum")
        ln_done, rinv_ready = sem("ln_done"), sem("rinv_ready")
        qk_ready = sem("qk_ready")
        bf_ready = sem("bf_ready")
        guard, negm_ready, diag_ready = sem("guard"), sem("negm_ready"), sem("diag_ready")
        rec_ready, lnden_done = sem("rec_ready"), sem("lnden_done")
        scored, exped, valued = sem("scored"), sem("exped"), sem("valued")
        o_ready, wo_done = sem("o_ready"), sem("wo_done")
        xa_ready, xb_ready = sem("xa_ready"), sem("xb_ready")
        f_mean, f_cen, f_sq, f_var = sem("f_mean"), sem("f_cen"), sem("f_sq"), sem("f_var")
        f_ln, f_rstd, f_xm, f_xn = sem("f_ln"), sem("f_rstd"), sem("f_xm"), sem("f_xn")
        f_up, f_gate, f_hid, f_down = sem("f_up"), sem("f_gate"), sem("f_hid"), sem("f_down")
        straight, fin, fin_sum, out_saved = sem("straight"), sem("fin"), sem("fin_sum"), sem("out_saved")
        block = ctx.enter_context(nc.Block())
        proj_bank = lambda n: bank((po, pS, pq)[n % 6 // 2], n % 2)
        QK_BLOCKS = [(0, 0, 64), (1, 64, 128)]

        def units(eng, first, middle, last, before, after, batch_start, batch_end):
            with eng.Fori(0, B) as b:
                batch_start(b)
                with eng.Fori(0, L) as l:
                    f = b * L + l
                    before(b, l, f)
                    first(f, f * NP, l)
                    with eng.Fori(1, NP) as i:
                        middle(f, f * NP + i, l, i)
                    last(f, f * NP + NP, l)
                    after(b, l, f)
                batch_end(b)

        @block.sync
        def _(sp):
            for started in (out_saved,):
                sp.nop().then_inc(started, 1)
            sp.dma_start(consts[:, :], cM).then_inc(const_in, 16)
            sp.dma_start(base[:, :, :], cB).then_inc(base_in, 16)
            sp.dma_start(wo_a[:, :], w_oA).then_inc(woa_in, 16)
            sp.dma_start(scales[:, :], par_d[0, :, 0:4]).then_inc(scales_in, 16)

            with sp.Fori(0, B) as b:
                sp.wait_ge(fin, 1 + b)
                for lo, hi, off in ((0, 64, 0), (64, 128, 1)):
                    sp.dma_start(xa[lo:hi, off:off + S], xnt_scr[b, lo:hi, :]).then_inc(xs_in, 16)
                sp.dma_start(oa[:, :], o_scr[b]).then_inc(oa_in, 16)
                sp.wait_ge(fin_sum, 1 + b)
                sp.dma_start(xtok[:, :, :], x[b].rearrange("(t p) d -> p t d", p=P)).then_inc(xtok_in, 16)
                with sp.Fori(0, L) as l:
                    f = b * L + l
                    u = f * NP
                    sp.wait_ge(wo_done, 1 + u)
                    sp.dma_start(wqk[:, :], w_pair[l * NP, :, 0:4 * P]).then_inc(wqk_in, 16)
                    sp.dma_start(wv[:, :], w_pair[l * NP, :, 4 * P:5 * P]).then_inc(wv_in, 16)
                    sp.dma_start(wo[:, :], w_oB[l * NP]).then_inc(wo_in, 16)
                    sp.wait_ge(table_ready, 1 + 4 * f + 4)
                    sp.dma_start(scales[:, :], par_d[l + 1, :, 0:4]).then_inc(scales_in, 16)
                    sp.wait_ge(filled, 1 + ITEMS * u + 8)
                    sp.dma_start(wqk[:, :], w_pair[l * NP + 1, :, 0:4 * P]).then_inc(wqk_in, 16)
                    sp.wait_ge(xa_ready, 1 + f)
                    sp.dma_start(par[:, :], par_d[l, :, 4:13]).then_inc(ffw_in, 16)
                    sp.dma_start(w1[:, :], w_1[l]).then_inc(ffw_in, 16)
                    sp.dma_start(w2[:, :, :], w_2[l].rearrange("(j p) d -> p j d", p=P)).then_inc(ffw_in, 16)
                    with sp.Fori(1, NP - 1) as i:
                        sp.wait_ge(filled, 1 + ITEMS * (u + i))
                        sp.dma_start(wv[:, :], w_pair[l * NP + i, :, 4 * P:5 * P]).then_inc(wv_in, 16)
                        sp.wait_ge(filled, 1 + ITEMS * (u + i) + 8)
                        sp.dma_start(wqk[:, :], w_pair[l * NP + i + 1, :, 0:4 * P]).then_inc(wqk_in, 16)
                        sp.wait_ge(wo_done, 1 + u + i)
                        sp.dma_start(wo[:, :], w_oB[l * NP + i]).then_inc(wo_in, 16)
                    sp.wait_ge(filled, 1 + ITEMS * (u + NP - 1))
                    sp.dma_start(wv[:, :], w_pair[l * NP + NP - 1, :, 4 * P:5 * P]).then_inc(wv_in, 16)
                    sp.wait_ge(wo_done, 1 + u + NP - 1)
                    sp.dma_start(wo[:, :], w_oB[l * NP + NP - 1]).then_inc(wo_in, 16)
                sp.wait_ge(fin_sum, 1 + b + 1)
                sp.dma_start(out[b].rearrange("(t p) d -> p t d", p=P), yout[:, :, :]).then_inc(out_saved, 16)
            sp.wait_ge(out_saved, 1 + 16 * B)

        @block.gpsimd
        def _(pool):
            for started in (rot_sum,):
                pool.nop().then_inc(started, 1)
            for t in (qp, qpb, dm):
                nc.gpsimd.memset(t[:, :, :], 0.0)
            nc.gpsimd.memset(kb[:, 0:WIN], 0.0)
            nc.gpsimd.memset(va[:, :, :, :], 1.0)
            nc.gpsimd.memset(onesb[:, :], 1.0)
            nc.gpsimd.memset(epsc[:, 0:1], EPS)
            nc.gpsimd.memset(epsc[:, 1:2], 12.0 * float(np.log(2.0)))
            nc.gpsimd.memset(zerob[:, :], 0.0).then_inc(pool_init, 1)
            pool.wait_ge(pool_init, 1)

            def add_rotated(u):
                for j in range(4):
                    pool.wait_ge(dve_read, 1 + ND * u + 2 * j + 2)
                    if j == 0:
                        pool.wait_ge(qk_ready, 1 + 6 * u)
                    nc.gpsimd.tensor_tensor(rsum[:, j, :], rcos[:, j, :], rsin[:, j, :], ALU.add).then_inc(rot_sum, 1)

            def diagonals(v):
                for part in range(2):
                    tiles = slice(part * T // 2, (part + 1) * T // 2)
                    pool.wait_ge(negm_ready, T * v + (part + 1) * T // 2)
                    if part == 0:
                        pool.wait_ge(dve_init, 1)
                    for h in range(2):
                        nc.gpsimd.tensor_tensor(dm[:, h, part * CH:(part + 1) * CH].rearrange("p (t n) -> p t n", n=P),
                                                identb[:, :].rearrange("p (o n) -> p o n", o=1).broadcast_to([P, T // 2, P]),
                                                negm[:, tiles, h:h + 1].broadcast_to([P, T // 2, P]),
                                                ALU.mult).then_inc(diag_ready, 1)

            def middle(f, u, l, i):
                add_rotated(u)
                diagonals(u - 1)

            none = lambda b: None
            units(pool, lambda f, u, l: add_rotated(u), middle, lambda f, u, l: diagonals(u - 1), lambda b, l, f: None, lambda b, l, f: None, none, none)

        @block.vector
        def _(dve):
            for started in (fin_sum, xa_ready, dve_read, o_ready, qk_ready,):
                dve.nop().then_inc(started, 1)
            dve.wait_ge(const_in, 16)
            nc.vector.memset(xa[64:128, 0:1], 0.0)
            nc.vector.memset(xb[64:128, 0:1], 0.0)
            nc.vector.tensor_copy(identb[:, :], ident)
            nc.vector.tensor_copy(mask[:, :, 0, :], cmask)
            nc.vector.tensor_copy(mask[:, :, 1, :], cmask).then_inc(dve_init, 1)

            def rotate(u, start):
                if start is not None:
                    dve.wait_ge(table_ready, 1 + 4 * start + 4)
                dve.wait_ge(rot_sum, 1 + 4 * u)
                for n in range(8):
                    dve.wait_ge(filled, 1 + ITEMS * u + n + 1)
                    c, k = n // 4, n % 4
                    dst = (rcos, rsin)[k % 2][:, 2 * c + k // 2, :]
                    nc.vector.tensor_tensor(dst, proj_bank(n), table[:, k, c * CH:(c + 1) * CH],
                                            ALU.mult).then_inc(dve_read, 1)

            def maxima(v):
                for qt in range(T):
                    dve.wait_ge(guard, T * v + qt + 1)
                    nc.vector.tensor_reduce(negm[:, qt, :], bank(pS, qt % 2)[:, 0:2 * SPAN].rearrange("p (h n) -> p h n", h=2),
                                            axis=AX.X, op=ALU.max, negate=True).then_inc(negm_ready, 1)

            def divide(v, half):
                src = (pq, po)[half]
                cols = slice(half * CH, (half + 1) * CH)
                dve.wait_ge(rec_ready, 2 * v + half + 1)
                nc.vector.tensor_tensor(ot[0:64, cols], src[0:64, 0:CH], rec[0:64, half, :], ALU.mult)
                nc.vector.tensor_tensor(ot[64:128, cols], src[64:128, CH:2 * CH], rec[64:128, half, :],
                                        ALU.mult).then_inc(o_ready, 1)

            def normalise(u):
                for n, j in enumerate((1, 3, 0, 2)):
                    c = j // 2
                    if n == 0:
                        dve.wait_ge(rinv_ready, 4 * u + 4)
                        dve.wait_ge(rot_sum, 1 + 4 * u + 4)
                        dve.wait_ge(scored, 1 + T * u)
                    if j % 2 == 0:
                        for h, lo, hi in QK_BLOCKS:
                            nc.vector.tensor_tensor(qp[lo:hi, h, c * CH:(c + 1) * CH], rsum[lo:hi, j, :],
                                                    rinv[lo:hi, j, :], ALU.mult).then_inc(qk_ready, 1)
                    else:
                        nc.vector.tensor_tensor(kk[:, c * CH:(c + 1) * CH], rsum[:, j, :], rinv[:, j, :],
                                                ALU.mult).then_inc(qk_ready, 1)

            def clamp(u):
                for j in range(4):
                    dve.wait_ge(filled, 1 + ITEMS * u + 8 + j + 1)
                    nc.vector.tensor_scalar(ssq[:, j, :], bank(pq, j % 2), 1e-24, None, ALU.max).then_inc(dve_read, 1)

            def first(f, u, l):
                rotate(u, f)
                clamp(u)
                normalise(u)

            def middle(f, u, l, i):
                rotate(u, None)
                maxima(u - 1)
                clamp(u)
                divide(u - 1, 0)
                divide(u - 1, 1)
                normalise(u)

            def last(f, u, l):
                maxima(u - 1)
                divide(u - 1, 0)
                divide(u - 1, 1)

            def after(b, l, f):
                dve.wait_ge(wo_done, 1 + NP * f + NP)
                for c in range(C):
                    for lo, hi, off in ((0, 64, 0), (64, 128, 1)):
                        cols = slice(c * CH + off, (c + 1) * CH + off)
                        ins = nc.vector.tensor_tensor(xb[lo:hi, cols], py[lo:hi, c * CH:(c + 1) * CH], xa[lo:hi, cols], ALU.add)
                ins.then_inc(xb_ready, 1)
                dve.wait_ge(xb_ready, f + 1)
                for c in range(C):
                    dve.wait_ge(f_mean, C * f + c + 1)
                    nc.vector.tensor_tensor(xcen[:, c * CH:(c + 1) * CH], xb[:, c * CH:(c + 1) * CH], bank(pq, c),
                                            ALU.subtract).then_inc(f_cen, 1)
                for c in range(C):
                    dve.wait_ge(f_rstd, C * f + c + 1)
                    if c == 0:
                        dve.wait_ge(f_cen, C * f + C)
                    nc.vector.tensor_tensor(xm[:, c * CH:(c + 1) * CH], xcen[:, c * CH:(c + 1) * CH],
                                            rstd[:, c * CH:(c + 1) * CH], ALU.mult).then_inc(f_xm, 1)
                for n in range(C * NJ):
                    c, j = n // NJ, n % NJ
                    dve.wait_ge(f_gate, C * NJ * f + n + 1)
                    nc.vector.scalar_tensor_tensor(hid[:, j, c * CH:(c + 1) * CH], (pq, pS)[n % 2][:, 0:CH],
                                                   par[:, 2 + j:3 + j], gate[:, n % 2, :], ALU.add, ALU.mult).then_inc(f_hid, 1)
                dve.wait_ge(f_down, C * f + C)
                for c in range(C):
                    for lo, hi, off in ((0, 64, 0), (64, 128, 1)):
                        cols = slice(c * CH + off, (c + 1) * CH + off)
                        ins = nc.vector.scalar_tensor_tensor(xa[lo:hi, cols], py[lo:hi, c * CH:(c + 1) * CH],
                                                             par[lo:hi, 8:9], xb[lo:hi, cols], ALU.add, ALU.add)
                ins.then_inc(xa_ready, 1)

            def batch_end(b):
                dve.wait_ge(xa_ready, 1 + L * b + L)
                for lo, hi, off in ((0, 64, 0), (64, 128, 1)):
                    ins = nc.vector.tensor_copy(ot[lo:hi, :], xa[lo:hi, off:off + S])
                ins.then_inc(straight, 1)
                dve.wait_ge(fin, 1 + b + 1)
                dve.wait_ge(xtok_in, 16 * b + 16)
                dve.wait_ge(out_saved, 1 + 16 * b)
                nc.vector.tensor_tensor(yout[:, :, :], pq[:, :].rearrange("p (t d) -> p t d", t=T), xtok[:, :, :],
                                        ALU.add).then_inc(fin_sum, 1)

            units(dve, first, middle, last, lambda b, l, f: None, after, lambda b: None, batch_end)

        @block.scalar
        def _(act):
            for started in (table_ready, act_read,):
                act.nop().then_inc(started, 1)
            act.wait_ge(pool_init, 1)

            def squares(u, js):
                for j in js:
                    n = (0, 2, 4, 6)[j]
                    act.wait_ge(dve_read, 1 + ND * u + n + 1)
                    nc.scalar.activation(sq[:, j, :], proj_bank(n), ACT.Square).then_inc(act_read, 1)

            def round_qk(u):
                act.wait_ge(qk_ready, 1 + 6 * u + 2)
                nc.scalar.activation(kb[:, WIN:WIN + S], kk[:, :], ACT.Copy).then_inc(bf_ready, 1)
                act.wait_ge(qk_ready, 1 + 6 * u + 6)
                for h, lo, hi in QK_BLOCKS:
                    ins = nc.scalar.activation(qpb[lo:hi, h, 0:S], qp[lo:hi, h, 0:S], ACT.Copy)
                ins.then_inc(bf_ready, 1)

            def exps(v, kts):
                for kt in kts:
                    act.wait_ge(scored, 1 + T * v + kt + 1)
                    nc.scalar.activation(prob[:, kt, :, :], bank(pS, kt % 2)[:, 0:2 * SPAN].rearrange("p (h n) -> p h n", h=2),
                                         ACT.Exp).then_inc(exped, 1)

            def invert(v, half):
                src = (pq, po)[half]
                act.wait_ge(valued, 2 * v + half + 1)
                nc.scalar.activation(lnden[0:64, half, :], src[64:128, 0:CH], ACT.Ln)
                nc.scalar.activation(lnden[64:128, half, :], src[0:64, CH:2 * CH], ACT.Ln).then_inc(lnden_done, 1)
                act.wait_ge(lnden_done, 2 * v + half + 1)
                nc.scalar.activation(rec[:, half, :], lnden[:, half, :], ACT.Exp, scale=-1.0).then_inc(rec_ready, 1)

            def norms(u):
                for j in range(4):
                    act.wait_ge(dve_read, 1 + ND * u + 8 + j + 1)
                    nc.scalar.activation(lnss[:, j, :], ssq[:, j, :], ACT.Ln, scale=2.0 ** 24).then_inc(ln_done, 1)
                for j in range(4):
                    act.wait_ge(ln_done, 4 * u + j + 1)
                    nc.scalar.activation(rinv[:, j, :], lnss[:, j, :], ACT.Exp, scale=-0.5,
                                         bias=epsc[:, 1:2]).then_inc(rinv_ready, 1)

            def take_v(u):
                for n in range(2):
                    act.wait_ge(filled, 1 + ITEMS * u + 12 + n + 1)
                    src = bank(pq, n).rearrange("p (t h d) -> p t h d", t=4, h=2)
                    for h in range(2):
                        ins = nc.scalar.activation(va[:, 4 * n:4 * n + 4, h, h * 64:h * 64 + 64], src[:, :, h, :], ACT.Copy)
                    ins.then_inc(act_read, 1)

            def first(f, u, l):
                squares(u, range(4))
                norms(u)
                take_v(u)
                round_qk(u)

            def middle(f, u, l, i):
                squares(u, range(4))
                norms(u)
                exps(u - 1, range(6))
                invert(u - 1, 0)
                exps(u - 1, range(6, T))
                invert(u - 1, 1)
                take_v(u)
                round_qk(u)

            def last(f, u, l):
                next_table(f + 1)
                exps(u - 1, range(6))
                invert(u - 1, 0)
                exps(u - 1, range(6, T))
                invert(u - 1, 1)

            def after(b, l, f):
                for c in range(C):
                    act.wait_ge(f_cen, C * f + c + 1)
                    nc.scalar.activation(xsq[:, c * CH:(c + 1) * CH], xcen[:, c * CH:(c + 1) * CH], ACT.Square).then_inc(f_sq, 1)
                for c in range(C):
                    act.wait_ge(f_var, C * f + c + 1)
                    nc.scalar.activation(lnvar[:, c * CH:(c + 1) * CH], bank(pS, c), ACT.Ln, bias=epsc[:, 0:1]).then_inc(f_ln, 1)
                for c in range(C):
                    act.wait_ge(f_ln, C * f + c + 1)
                    nc.scalar.activation(rstd[:, c * CH:(c + 1) * CH], lnvar[:, c * CH:(c + 1) * CH], ACT.Exp,
                                         scale=-0.5).then_inc(f_rstd, 1)
                for c in range(C):
                    act.wait_ge(f_xm, C * f + c + 1)
                    if c == 0:
                        act.wait_ge(ffw_in, 48 * f + 48)
                    nc.scalar.activation(xnn[:, c * CH:(c + 1) * CH], xm[:, c * CH:(c + 1) * CH], ACT.Identity,
                                         scale=par[:, 0:1], bias=par[:, 1:2]).then_inc(f_xn, 1)
                for n in range(C * NJ):
                    j = n % NJ
                    act.wait_ge(f_up, C * NJ * f + n + 1)
                    nc.scalar.activation(gate[:, n % 2, :], (pq, pS)[n % 2][:, CH:2 * CH], ACT.Gelu,
                                         bias=par[:, 5 + j:6 + j]).then_inc(f_gate, 1)

            def before(b, l, f):
                nc.scalar.preload_act_table_set(EXP_LN_SET)

            def next_table(f):
                act.wait_ge(base_in, 16)
                act.wait_ge(scales_in, 16 * f + 16)
                act.wait_ge(dve_read, 1 + ND * NP * f)
                for k in range(4):
                    nc.scalar.activation(table[:, k, :], base[:, k, :], ACT.Copy, scale=scales[:, k:k + 1]).then_inc(table_ready, 1)

            next_table(0)
            units(act, first, middle, last, before, after, lambda b: None, lambda b: None)

        @block.tensor
        def _(pe):
            for started in (fin, filled, wo_done, scored,):
                pe.nop().then_inc(started, 1)
            pe.wait_ge(pool_init, 1)
            pe.wait_ge(dve_init, 1)
            pe.wait_ge(const_in, 16)
            pe.wait_ge(woa_in, 16)

            def project_qk(u):
                pe.wait_ge(wqk_in, 16 * u + 16)
                pe.wait_ge(dve_read, 1 + ND * u)
                for n in range(8):
                    if n >= 6:
                        pe.wait_ge(dve_read, 1 + ND * u + upto(DVE_ITEMS, n - 6))
                        pe.wait_ge(act_read, 1 + NA * u + upto(ACT_ITEMS, n - 6))
                    elif n == 4:
                        pe.wait_ge(act_read, 1 + NA * u)
                    c, k = n // 4, n % 4
                    nc.tensor.matmul(proj_bank(n), wqk[:, k * P:(k + 1) * P], xa[:, c * CH:(c + 1) * CH],
                                     start=True, stop=True).then_inc(filled, 1)

            def norms(u):
                pe.wait_ge(dve_read, 1 + ND * u + 8)
                pe.wait_ge(act_read, 1 + NA * u + 4)
                for j in range(4):
                    if j >= 2:
                        pe.wait_ge(dve_read, 1 + ND * u + 8 + j - 1)
                    nc.tensor.matmul(bank(pq, j % 2), pairsum, sq[:, j, :], start=True, stop=True).then_inc(filled, 1)

            def project_v(u, v):
                pe.wait_ge(wv_in, 16 * u + 16)
                if v is None:
                    pe.wait_ge(dve_read, 1 + ND * u + ND)
                else:
                    pe.wait_ge(o_ready, 1 + 2 * v + 1)
                for n in range(2):
                    for t in range(4):
                        tt = 4 * n + t
                        last = nc.tensor.matmul(bank(pq, n)[:, t * P:(t + 1) * P], xa[:, tt * P:(tt + 1) * P], wv[:, :],
                                                start=True, stop=True)
                    last.then_inc(filled, 1)

            def maxima(v, read):
                pe.wait_ge(bf_ready, 2 * v + 2)
                read()
                for qt in range(T):
                    if qt >= 2:
                        pe.wait_ge(negm_ready, T * v + qt - 1)
                    dst = bank(pS, qt % 2)
                    for h in range(2):
                        nc.tensor.matmul(dst[:, h * SPAN:(h + 1) * SPAN], qpb[:, h, qt * P:(qt + 1) * P],
                                         kb[:, qt * P:qt * P + SPAN], start=(h == 0), stop=False, skip_group_check=True)
                    nc.tensor.matmul(dst[:, 0:2 * SPAN], identb[:, :], mask[:, 2 if qt == 0 else 1, :, :],
                                     start=False, stop=True, skip_group_check=True).then_inc(guard, 1)

            def attend(v, pq_free):
                def score(kt):
                    if kt < 2:
                        pe.wait_ge(negm_ready, T * v + T - 1 + kt)
                    else:
                        pe.wait_ge(exped, T * v + kt - 1)
                    dst = bank(pS, kt % 2)[:, 0:2 * SPAN]
                    nc.tensor.matmul(dst, kk[:, kt * P:(kt + 1) * P], qp[:, :, kt * P:kt * P + SPAN],
                                     start=True, stop=False)
                    nc.tensor.matmul(dst, identb[:, :], mask[:, 0, :, :], start=False, stop=False)
                    if kt in (0, 3):
                        pe.wait_ge(diag_ready, 4 * v + (2 if kt == 0 else 4))
                    nc.tensor.matmul(dst, onesb[:, :], dm[:, :, kt * P:kt * P + SPAN], start=False,
                                     stop=True).then_inc(scored, 1)

                def values(kt):
                    pe.wait_ge(exped, T * v + kt + 1)
                    if kt == 0:
                        pe.wait_ge(act_read, 1 + NA * v + NA)
                        pq_free()
                    if kt == 3:
                        pe.wait_ge(o_ready, 1 + 2 * v)
                    for half, dst in ((0, pq), (1, po)):
                        lo, hi = max(kt * P, half * CH), min(kt * P + SPAN, (half + 1) * CH)
                        if lo >= hi:
                            continue
                        for h in range(2):
                            last = nc.tensor.matmul(bank(dst, h)[:, lo - half * CH:hi - half * CH], va[:, kt, h, :],
                                                    prob[:, kt, h, lo - kt * P:hi - kt * P],
                                                    start=(kt == (0, 3)[half]), stop=False, skip_group_check=True)
                        if (half, kt) in ((0, 3), (1, 7)):
                            last.then_inc(valued, 1)

                score(0)
                for kt in range(T):
                    if kt + 1 < T:
                        score(kt + 1)
                    values(kt)

            def project_out(v):
                pe.wait_ge(o_ready, 1 + 2 * v + 2)
                pe.wait_ge(wo_in, 16 * v + 16)
                for c in range(C):
                    last = nc.tensor.matmul(bank(py, c), wo[:, :], ot[:, c * CH:(c + 1) * CH], start=False, stop=False,
                                            skip_group_check=True)
                last.then_inc(wo_done, 1)

            def batch_start(b):
                pass

            def before(b, l, f):
                pe.wait_ge(xa_ready, 1 + f)
                pe.wait_ge(xs_in, 32 * b + 32)
                pe.wait_ge(fin_sum, 1 + b)
                for c in range(C):
                    nc.tensor.matmul(bank(py, c)[:, 0:2 * SPAN], zerob[:, :], mask[:, 0, :, :], start=True, stop=False,
                                     skip_group_check=True)
                    nc.tensor.matmul(bank(py, c)[:, 2 * SPAN:CH], zerob[:, :], dm[:, 0, 0:CH - 2 * SPAN], start=False,
                                     stop=False, skip_group_check=True)

            def first(f, u, l):
                project_qk(u)
                norms(u)
                project_v(u, None)

            def middle(f, u, l, i):
                v = u - 1
                project_qk(u)
                maxima(v, lambda: (pe.wait_ge(dve_read, 1 + ND * u + 8), pe.wait_ge(act_read, 1 + NA * u + 4)))
                norms(u)
                attend(v, lambda: pe.wait_ge(dve_read, 1 + ND * u + ND))
                project_v(u, v)
                project_out(v)

            def last(f, u, l):
                v = u - 1
                maxima(v, lambda: pe.wait_ge(act_read, 1 + NA * v + NA))
                attend(v, lambda: None)
                project_out(v)

            def after(b, l, f):
                pe.wait_ge(xb_ready, f + 1)
                for c in range(C):
                    nc.tensor.matmul(bank(pq, c), mean_w, xb[:, c * CH:(c + 1) * CH], start=True, stop=True).then_inc(f_mean, 1)
                for c in range(C):
                    pe.wait_ge(f_sq, C * f + c + 1)
                    nc.tensor.matmul(bank(pS, c), mean_w, xsq[:, c * CH:(c + 1) * CH], start=True, stop=True).then_inc(f_var, 1)
                pe.wait_ge(f_xn, C * f + C)
                pe.wait_ge(ffw_in, 48 * f + 48)
                for n in range(C * NJ):
                    c, j = n // NJ, n % NJ
                    if n >= 2:
                        pe.wait_ge(f_hid, C * NJ * f + n - 1)
                    for k in range(2):
                        last = nc.tensor.matmul((pq, pS)[n % 2][:, k * CH:(k + 1) * CH],
                                                w1[:, k * DIP + j * P:k * DIP + (j + 1) * P],
                                                xnn[:, c * CH:(c + 1) * CH], start=True, stop=True)
                    last.then_inc(f_up, 1)
                for c in range(C):
                    pe.wait_ge(f_hid, C * NJ * f + (c + 1) * NJ)
                    for j in range(NJ):
                        last = nc.tensor.matmul(bank(py, c), w2[:, j, :], hid[:, j, c * CH:(c + 1) * CH],
                                                start=(j == 0), stop=(j == NJ - 1))
                    last.then_inc(f_down, 1)

            def batch_end(b):
                pe.wait_ge(straight, b + 1)
                pe.wait_ge(oa_in, 16 * b + 16)
                for t in range(T):
                    dst = pq[:, t * P:(t + 1) * P]
                    nc.tensor.matmul(dst, oa[:, t * P:(t + 1) * P], wo_a[:, :], start=(t % 4 == 0), stop=False,
                                     skip_group_check=True)
                    last = nc.tensor.matmul(dst, ot[:, t * P:(t + 1) * P], ident, start=False, stop=False,
                                            skip_group_check=True)
                last.then_inc(fin, 1)

            units(pe, first, middle, last, before, after, batch_start, batch_end)


def build(nc, a, out):
    o_scr = nc.dram_tensor("o_scr", (B, D, S), F32).ap()
    xnt_scr = nc.dram_tensor("xnt_scr", (B, D, S), F32).ap()
    part_scr = nc.dram_tensor("part_scr", (2, 3, D, S), BF16).ap()
    m_scr = nc.dram_tensor("m_scr", (P, P), BF16).ap()
    branch_a(nc, a["x"], a["wA"], a["cA"], a["cM"][:, 0:P], a["cM"][:, CONSTS - P:CONSTS], o_scr, xnt_scr, part_scr, m_scr)
    branch_b(nc, a["x"], a["w_pair"], a["w_oB"], a["w_1"], a["w_2"], a["par"], a["cB"], a["cM"], a["w_oA"],
             xnt_scr, o_scr, out)


def position_constants():
    f = np.float32
    t = np.arange(S, dtype=f)
    inv = f(10000.0) ** (-(np.arange(DA // 2, dtype=f) * f(2.0) / f(DA)))
    ang = (t[:, None] * inv[None, :]).astype(f)
    d = np.arange(DA)
    sign = np.where(d % 2 == 0, f(-1), f(1))
    cA = np.stack([np.tile(np.cos(ang)[:, d // 2].T, (HA, 1)),
                   np.tile((np.sin(ang)[:, d // 2] * sign).T, (HA, 1))], 1).astype(f)
    half = np.arange(0, DB, 2, dtype=f)
    inv = (f(1.0) / f(10000.0) ** (half / f(DB))).astype(f)
    fr = (t[:, None] * inv[None, :]).astype(f)
    base = ((half + f(0.4 * DB)) / f(1.4 * DB)).astype(f)
    power = ((t - f(S // 2)) / f(WIN // 2)).astype(f)
    sc = (base[None, :] ** power[:, None]).astype(f)
    fr, sc = np.concatenate([fr, fr], -1), np.concatenate([sc, sc], -1)
    sign = np.where(np.arange(DB) < DB // 2, f(-1), f(1))[None, :]
    isc = (f(1.0) / sc).astype(f)
    tabs = [np.cos(fr) * sc * f(8), np.sin(fr) * sc * sign * f(8), np.cos(fr) * isc, np.sin(fr) * isc * sign]
    cB = np.stack([np.tile(x.T, (2, 1)) for x in tabs], 1).astype(f)
    p, n = np.arange(P)[:, None], np.arange(SPAN)[None, :]
    off = f(-1e30)
    by_key = np.where((n >= p) & (n <= p + WIN), f(0), off)
    by_query = by_key
    first = np.where(n < WIN, off, by_query)
    pair = (np.arange(P)[:, None] // DB == np.arange(P)[None, :] // DB).astype(f)
    cM = np.concatenate([np.eye(P, dtype=f), pair, np.full((P, P), f(1.0 / D)), by_key, by_query, first,
                         np.triu(np.ones((P, P), f))], 1).astype(f)
    return np.ascontiguousarray(cA), np.ascontiguousarray(cB), np.ascontiguousarray(cM)


def lay_out(i):
    c = np.ascontiguousarray
    swap = np.arange(D) ^ 1
    wq, wk, wv = (np.asarray(i[f"L0_attn_w_{n}"]).T for n in "qkv")
    wA = c(np.concatenate([wq, wq[:, swap], wk, wk[:, swap], wv], 1))
    W = np.asarray(i["L0_ffn_Wqkv"]).reshape(L, D, 3, NP, 2, DB)
    rot = np.concatenate([np.arange(DB // 2, DB), np.arange(DB // 2)])
    q, k, v = (W[:, :, n].transpose(0, 2, 1, 3, 4) for n in range(3))
    w_pair = c(np.stack([q, q[..., rot], k, k[..., rot], v], 3).reshape(L * NP, D, 5 * P))
    w_oB = c(np.asarray(i["L0_ffn_Wo"]).reshape(L * NP, P, D))
    pad = ((0, 0), (0, 0), (0, DIP - DI))
    W1 = np.asarray(i["L0_ffn_W1"])
    w_1 = c(np.concatenate([np.pad(W1[:, :, :DI], pad), np.pad(W1[:, :, DI:], pad)], 2))
    w_2 = c(np.pad(np.asarray(i["L0_ffn_W2"]), ((0, 0), (0, DIP - DI), (0, 0))))
    qs, ks = np.asarray(i["L0_ffn_q_scale"]), np.asarray(i["L0_ffn_k_scale"])
    two = lambda s: np.concatenate([s, s], 1)[:, :, None]
    b1 = np.asarray(i["L0_ffn_b1"])
    cols = lambda s: np.pad(s, ((0, 0), (0, DIP - DI))).reshape(L, NJ, P).transpose(0, 2, 1)
    par = c(np.concatenate([two(qs), two(qs[:, rot]), two(ks), two(ks[:, rot]),
                            np.asarray(i["L0_ffn_ln_g"])[:, :, None], np.asarray(i["L0_ffn_ln_b"])[:, :, None],
                            cols(b1[:, :DI]), cols(b1[:, DI:]), np.asarray(i["L0_ffn_b2"])[:, :, None]], 2))
    par = c(np.concatenate([par, par[:1]], 0))
    cA, cB, cM = position_constants()
    return {"x": c(np.asarray(i["L0_attn_x"])), "wA": wA, "w_oA": c(np.asarray(i["L0_attn_w_o"]).T), "w_pair": w_pair,
            "w_oB": w_oB, "w_1": w_1, "w_2": w_2, "par": par, "cA": cA, "cB": cB, "cM": cM}


def kernel(**inputs):
    import concourse.bacc as bacc
    from concourse.bass_utils import run_bass_kernel_spmd

    nc = bacc.Bacc("TRN2", target_bir_lowering=False, num_devices=1)
    arrays = lay_out(inputs)
    aps = {n: nc.dram_tensor(f"in_{n}", v.shape, mybir.dt.from_np(v.dtype), kind="ExternalInput").ap()
           for n, v in arrays.items()}
    out = nc.dram_tensor("out", (B, S, D), F32, kind="ExternalOutput").ap()
    build(nc, aps, out)
    r = run_bass_kernel_spmd(nc, [{f"in_{n}": v for n, v in arrays.items()}], core_ids=[0])
    return r.results[0]["out"]
```

```python
import numpy as np
import concourse.bass as bass
from concourse import mybir
from contextlib import ExitStack

F32 = mybir.dt.float32
BF16 = mybir.dt.bfloat16
ACT = mybir.ActivationFunctionType
ALU = mybir.AluOpType
AX = mybir.AxisListType

B, S, D = 4, 1024, 128
P = 128
T = S // P
CH = 512
C = S // CH
HA, DA = 16, 8
SCALE_A = 1.0 / float(np.sqrt(DA))
TERMS_Q = [0, 0, 1, 1, 0, 2]
TERMS_K = [0, 1, 0, 1, 2, 0]
HALF_TAKEN = (2, 6)
SHIFT_ROW = 96
EPS = 1e-5
L, HB, DB, WIN = 6, 16, 64, 32
NP = HB // 2
SPAN = P + WIN
DI = 341
NJ = 3
DIP = NJ * P
EXP_LN_SET = "natural_log_exp_and_others"
CONSTS = 3 * P + 32 + 3 * SPAN
ITEMS, ACT_ITEMS = 7, 6
BCAST = 2

def branch_a(nc, x, wA, cA, ident_d, causal_d, o_scr, xnt_scr, part_scr, m_scr):
    with ExitStack() as ctx:
        sb = lambda n, s, d=F32: ctx.enter_context(nc.sbuf_tensor(n, s, d))
        ps = lambda n: ctx.enter_context(nc.psum_tensor(n, [P, S], F32))
        sem = lambda n: ctx.enter_context(nc.semaphore(n))
        ident = sb("a_ident", [P, P])
        w = sb("a_w", [P, 5 * D])
        causal = sb("a_causal", [P, P])
        rope = sb("a_rope", [P, 2, S])
        xtok = sb("a_xtok", [P, T, D])
        xc = sb("a_xc", [P, T, D])
        sq = sb("a_sq", [P, T, D])
        mean, var, rstd = sb("a_mean", [P, T]), sb("a_var", [P, T]), sb("a_rstd", [P, T])
        std = sb("a_std", [P, T])
        xn = sb("a_xn", [P, T, D])
        xnt = sb("a_xnt", [P, S])
        cosq = sb("a_cosq", [P, 2, S])
        sinq = sb("a_sinq", [P, 2, S])
        rest = sb("a_rest", [P, 2, S])
        parts = sb("a_parts", [P, 2, 3, S], BF16)
        v = sb("a_v", [P, T, D])
        qs = sb("a_qstack", [P, HA * S], BF16)
        ks = sb("a_kstack", [P, HA * S], BF16)
        negm = sb("a_negm", [P, HA * T])
        low = sb("a_low", [P, 4, S], BF16)
        larger, half2, half3 = (sb(n, [P, T, w], BF16) for n, w in (("a_larger", CH), ("a_half2", CH // 2), ("a_half3", CH // 4)))
        negmt = sb("a_negmt", [P, P], BF16)
        vh = sb("a_vh", [P, 2, T, 32])
        ones = sb("a_ones", [P, 32])
        prob = sb("a_prob", [P, 4, S])
        diag = sb("a_diag", [P, 2, P])
        rec = sb("a_rec", [64, 2, CH])
        oh = sb("a_oh", [64, 2, CH])
        banks = [ps(f"a_ps{i}") for i in range(4)]

        const_in, w_in = sem("a_const_in"), sem("a_w_in")
        x_in, xnt_saved = sem("a_x_in"), sem("a_xnt_saved")
        zeroed = sem("a_zeroed")
        ln = sem("a_ln")
        std_done = sem("a_std_done")
        transposed, xnt_ready = sem("a_transposed"), sem("a_xnt_ready")
        proj, rot = sem("a_proj"), sem("a_rot")
        v_proj, v_ready = sem("a_v_proj"), sem("a_v_ready")
        rotated = sem("a_rotated")
        split = sem("a_split")
        parts_out, stacks_in = sem("a_parts_out"), sem("a_stacks_in")
        guard, guard_max = sem("a_guard"), sem("a_guard_max")
        low_ready, larger_ready, halved = sem("a_low_ready"), sem("a_larger_ready"), sem("a_halved")
        m_trans, m_ready = sem("a_m_trans"), sem("a_m_ready")
        m_out, m_in = sem("a_m_out"), sem("a_m_in")
        scored, exped, masked, summed = sem("a_scored"), sem("a_exped"), sem("a_masked"), sem("a_summed")
        vh_ready, recd = sem("a_vh_ready"), sem("a_recd")
        normed = [sem("a_normed0"), sem("a_normed1")]
        o_saved = [sem("a_o_saved0"), sem("a_o_saved1")]
        block = ctx.enter_context(nc.Block())
        NDMA_STACK = 16 * 2 * len(TERMS_Q)

        @block.sync
        def _(sp):
            for started in (xnt_saved, parts_out, m_out, o_saved[0], o_saved[1],):
                sp.nop().then_inc(started, 1)
            sp.dma_start(ident[:, :], ident_d).then_inc(const_in, 16)
            sp.dma_start(causal[:, :], causal_d).then_inc(const_in, 16)
            sp.dma_start(rope[:, :, :], cA).then_inc(const_in, 16)
            sp.dma_start(w[:, :], wA).then_inc(w_in, 16)
            with sp.Fori(0, B) as b:
                sp.wait_ge(ln, 1 + 7 * b)
                sp.dma_start(xtok[:, :, :], x[b].rearrange("(t p) d -> p t d", p=P)).then_inc(x_in, 16)
                sp.wait_ge(xnt_ready, b + 1)
                sp.dma_start(xnt_scr[b], xnt[:, :]).then_inc(xnt_saved, 16)
                sp.wait_ge(zeroed, 4)
                for done, group in ((1, (0,)), (3, (1, 2))):
                    for part in group:
                        for side in range(2):
                            sp.wait_ge(split, 6 * b + 2 * part + side + 1)
                            sp.dma_start(part_scr[side, part], parts[:, side, part, :]).then_inc(parts_out, 16)
                    sp.wait_ge(parts_out, 1 + 96 * b + 32 * done)
                    for stack, side, terms in ((qs, 0, TERMS_Q), (ks, 1, TERMS_K)):
                        for t, part in enumerate(terms):
                            if part in group:
                                sp.dma_start(stack[DA * t:DA * t + DA, :].rearrange("r (h n) -> r h n", h=HA),
                                             part_scr[side, part].rearrange("(h r) n -> r h n", r=DA)).then_inc(stacks_in, 16)
                sp.wait_ge(m_ready, b + 1)
                sp.dma_start(m_scr, negmt[:, :]).then_inc(m_out, 16)
                sp.wait_ge(m_out, 1 + 16 * b + 16)
                sp.dma_start(qs[SHIFT_ROW:SHIFT_ROW + 1, :], m_scr.rearrange("(a m) n -> a (m n)", a=1)).then_inc(m_in, 16)
                with sp.Fori(0, HA // 2) as hh:
                    for par in range(2):
                        g = b * (HA // 2) + hh
                        sp.wait_ge(normed[par], 1 + g + 1)
                        for c in range(C):
                            sp.dma_start(o_scr[b, bass.ds((2 * hh + par) * DA, DA), c * CH:(c + 1) * CH],
                                         oh[32 * c:32 * c + DA, par, :]).then_inc(o_saved[par], 16)
            sp.wait_ge(xnt_saved, 1 + 16 * B)
            for par in range(2):
                sp.wait_ge(o_saved[par], 1 + 32 * B * HA // 2)

        @block.gpsimd
        def _(pool):
            nc.gpsimd.memset(qs[:, :], 0.0).then_inc(zeroed, 1)
            nc.gpsimd.memset(ks[:, :], 1.0).then_inc(zeroed, 1)
            nc.gpsimd.memset(vh[:, :, :, :], 0.0).then_inc(zeroed, 1)
            nc.gpsimd.memset(ones[:, :], 1.0).then_inc(zeroed, 1)
            pool.wait_ge(zeroed, 4)
            pool.wait_ge(const_in, 48)
            with pool.Fori(0, B) as b:
                with pool.Fori(0, HA // 2) as hh:
                    for par in range(2):
                        h = 2 * hh + par
                        g = b * HA + h
                        pool.wait_ge(v_ready, b + 1)
                        nc.gpsimd.tensor_copy(vh[:, par, :, 0:DA], v[:, :, bass.ds(h * DA, DA)]).then_inc(vh_ready, 1)
                        for kt in range(T):
                            pool.wait_ge(exped, 8 * g + kt + 1)
                            pool.wait_ge(summed, 8 * g + kt + 3)
                            nc.gpsimd.tensor_tensor(diag[:, kt % 2, :], prob[:, kt % 4, kt * P:(kt + 1) * P], causal[:, :],
                                                    ALU.mult).then_inc(masked, 1)

        @block.vector
        def _(dve):
            for started in (ln, guard_max, halved, normed[0], normed[1]):
                dve.nop().then_inc(started, 1)
            dve.nop().then_inc(larger_ready, 4)
            with dve.Fori(0, B) as b:
                dve.wait_ge(x_in, 16 * b + 16)
                dve.wait_ge(transposed, 1 + b)
                n = 7 * b
                bc = lambda t: t[:, :].rearrange("p (t o) -> p t o", o=1).broadcast_to([P, T, D])
                nc.vector.tensor_reduce(mean[:, :], xtok[:, :, :], axis=AX.X, op=ALU.add).then_inc(ln, 1)
                dve.wait_ge(ln, 1 + n + 1)
                nc.vector.tensor_scalar(mean[:, :], mean[:, :], 1.0 / D, None, ALU.mult).then_inc(ln, 1)
                dve.wait_ge(ln, 1 + n + 2)
                nc.vector.tensor_tensor(xc[:, :, :], xtok[:, :, :], bc(mean), ALU.subtract).then_inc(ln, 1)
                dve.wait_ge(ln, 1 + n + 3)
                nc.vector.tensor_tensor(sq[:, :, :], xc[:, :, :], xc[:, :, :], ALU.mult).then_inc(ln, 1)
                dve.wait_ge(ln, 1 + n + 4)
                nc.vector.tensor_reduce(var[:, :], sq[:, :, :], axis=AX.X, op=ALU.add).then_inc(ln, 1)
                dve.wait_ge(ln, 1 + n + 5)
                nc.vector.tensor_scalar(var[:, :], var[:, :], 1.0 / D, EPS, ALU.mult, ALU.add).then_inc(ln, 1)
                dve.wait_ge(std_done, b + 1)
                nc.vector.reciprocal(rstd[:, :], std[:, :]).then_inc(ln, 1)
                dve.wait_ge(ln, 1 + n + 7)
                nc.vector.tensor_tensor(xn[:, :, :], xc[:, :, :], bc(rstd), ALU.mult).then_inc(recd, 1)
                dve.wait_ge(transposed, 1 + b + 1)
                dve.wait_ge(xnt_saved, 1 + 16 * b)
                nc.vector.tensor_copy(xnt[:, :], banks[0][:, :]).then_inc(xnt_ready, 1)
                dve.wait_ge(const_in, 48)
                for side in range(2):
                    for k, dst in ((0, cosq), (1, sinq)):
                        n4 = 2 * side + k
                        dve.wait_ge(proj, 8 * b + 2 * n4 + 2)
                        nc.vector.tensor_tensor(dst[:, side, :], banks[(n4 + 1) % 4][:, :], rope[:, k, :],
                                                ALU.mult).then_inc(rot, 1)
                for side in range(2):
                    dve.wait_ge(rot, 4 * b + 2 * side + 2)
                    nc.vector.tensor_tensor(rest[:, side, :], cosq[:, side, :], sinq[:, side, :], ALU.add).then_inc(rotated, 1)
                for step in range(2):
                    for side in range(2):
                        dve.wait_ge(split, 6 * b + 2 * step + side + 1)
                        dve.wait_ge(rotated, 6 * b + 2 * step + side + 1)
                        nc.vector.tensor_tensor(rest[:, side, :], rest[:, side, :], parts[:, side, step, :],
                                                ALU.subtract).then_inc(rotated, 1)

                def shrink(n, h, group, step):
                    tiles = slice(4 * group, 4 * group + 4)
                    if step == 0:
                        dve.wait_ge(larger_ready, 4 + 4 * n + 4)
                        nc.vector.tensor_tensor(half2[:, tiles, :], larger[:, tiles, 0:CH // 2], larger[:, tiles, CH // 2:CH],
                                                ALU.max).then_inc(halved, 1)
                    elif step == 1:
                        dve.wait_ge(halved, 1 + 2 * n + 1)
                        dve.wait_ge(guard_max, 1 + n)
                        nc.vector.tensor_tensor(half3[:, tiles, :], half2[:, tiles, 0:CH // 4],
                                                half2[:, tiles, CH // 4:CH // 2], ALU.max).then_inc(halved, 1)
                    else:
                        dve.wait_ge(halved, 1 + 2 * n + 2)
                        nc.vector.tensor_reduce(negm[:, bass.ds(h * T + 4 * group, 4)], half3[:, tiles, :], axis=AX.X,
                                                op=ALU.max, negate=True).then_inc(guard_max, 1)

                def guard_head(h, first=False):
                    g = b * HA + h
                    for group in range(2):
                        n = 2 * g + group
                        for qt in range(4 * group, 4 * group + 4):
                            dve.wait_ge(low_ready, 8 * g + qt + 1)
                            if qt == 4 * group and not (first and group == 0):
                                dve.wait_ge(halved, 2 * n - 1)
                            head = banks[qt % 4][:, 0:CH] if qt in HALF_TAKEN else low[:, qt % 4, 0:CH]
                            nc.vector.tensor_tensor(larger[:, qt, :], head, low[:, qt % 4, CH:2 * CH],
                                                    ALU.max).then_inc(larger_ready, 1)
                            step = qt - 4 * group
                            if step < 3 and not (first and group == 0):
                                shrink(n - 1, h if group else h - 1, 1 - group, step)

                guard_head(0, first=True)
                with dve.Fori(1, HA) as h:
                    guard_head(h)
                for step in range(3):
                    shrink(2 * HA * b + 2 * HA - 1, HA - 1, 1, step)
                dve.wait_ge(m_trans, b + 1)
                dve.wait_ge(m_out, 1 + 16 * b)
                nc.vector.tensor_copy(negmt[:, :], banks[0][:, 0:P]).then_inc(m_ready, 1)
                with dve.Fori(0, HA // 2) as hh:
                    g = b * (HA // 2) + hh
                    for par in range(2):
                        acc = banks[2 + par]
                        dve.wait_ge(summed, 4 + 8 * (2 * g + par) + 8)
                        dve.wait_ge(normed[par], 1 + g)
                        nc.vector.reciprocal(rec[:, par, :], acc[64:128, 0:CH]).then_inc(recd, 1)
                        dve.wait_ge(recd, b + 2 * g + par + 2)
                        dve.wait_ge(o_saved[par], 1 + 32 * g)
                        nc.vector.tensor_tensor(oh[:, par, :], acc[0:64, 0:CH], rec[:, par, :], ALU.mult).then_inc(normed[par], 1)

        @block.scalar
        def _(act):
            with act.Fori(0, B) as b:
                act.wait_ge(ln, 1 + 7 * b + 6)
                nc.scalar.activation(std[:, :], var[:, :], ACT.Sqrt).then_inc(std_done, 1)
                nc.scalar.preload_act_table_set("exp_and_others")
                for part in range(3):
                    for side in range(2):
                        if part == 0:
                            act.wait_ge(parts_out, 1 + 96 * b)
                        act.wait_ge(rotated, 6 * b + 2 * part + side + 1)
                        nc.scalar.activation(parts[:, side, part, :], rest[:, side, :], ACT.Copy).then_inc(split, 1)
                act.wait_ge(v_proj, b + 1)
                nc.scalar.activation(v[:, :, :], banks[0][:, :].rearrange("p (t d) -> p t d", t=T), ACT.Copy).then_inc(v_ready, 1)
                with act.Fori(0, HA) as h:
                    g = b * HA + h
                    for qt in range(T):
                        act.wait_ge(guard, 8 * g + qt + 1)
                        act.wait_ge(larger_ready, 8 * g + qt + 1)
                        c0 = CH if qt in HALF_TAKEN else 0
                        nc.scalar.activation(low[:, qt % 4, c0:S], banks[qt % 4][:, c0:S], ACT.Copy).then_inc(low_ready, 1)
                with act.Fori(0, HA) as h:
                    g = b * HA + h
                    for kt in range(T):
                        act.wait_ge(scored, 8 * g + kt + 1)
                        act.wait_ge(summed, 8 * g + kt + 1)
                        nc.scalar.activation(prob[:, kt % 4, :], banks[kt % 2][:, :], ACT.Exp, scale=SCALE_A).then_inc(exped, 1)

        @block.tensor
        def _(pe):
            pe.nop().then_inc(transposed, 1)
            pe.nop().then_inc(summed, 4)
            pe.wait_ge(const_in, 48)
            pe.wait_ge(w_in, 16)
            with pe.Fori(0, B) as b:
                pe.wait_ge(recd, b * (HA + 1) + 1)
                for t in range(T):
                    last = nc.tensor.transpose(banks[0][:, t * P:(t + 1) * P], xn[:, t, :], ident[:, :])
                last.then_inc(transposed, 1)
                pe.wait_ge(xnt_ready, b + 1)
                for n in range(4):
                    for c in range(C):
                        nc.tensor.matmul(banks[(n + 1) % 4][:, c * CH:(c + 1) * CH], w[:, n * D:(n + 1) * D],
                                         xnt[:, c * CH:(c + 1) * CH], start=True, stop=True).then_inc(proj, 1)
                pe.wait_ge(rot, 4 * b + 4)
                for t in range(T):
                    last = nc.tensor.matmul(banks[0][:, t * P:(t + 1) * P], xnt[:, t * P:(t + 1) * P],
                                            w[:, 4 * D:5 * D], start=True, stop=True)
                last.then_inc(v_proj, 1)
                with pe.Fori(0, HA) as h:
                    g = b * HA + h
                    pe.wait_ge(zeroed, 4)
                    pe.wait_ge(v_ready, b + 1)
                    pe.wait_ge(stacks_in, NDMA_STACK * (b + 1))
                    for qt in range(T):
                        pe.wait_ge(larger_ready, 8 * g + qt + 1)
                        for c in range(C):
                            last = nc.tensor.matmul(banks[qt % 4][:, c * CH:(c + 1) * CH],
                                                    qs[0:SHIFT_ROW, bass.ds(h * S + qt * P, P)],
                                                    ks[0:SHIFT_ROW, bass.ds(h * S + c * CH, CH)], start=True, stop=True)
                        last.then_inc(guard, 1)
                pe.wait_ge(guard_max, 1 + 2 * HA * (b + 1))
                nc.tensor.transpose(banks[0][:, 0:P], negm[:, :], ident[:, :]).then_inc(m_trans, 1)
                def score(h, kt, first=False):
                    g = b * HA + h
                    if not first:
                        pe.wait_ge(exped, 8 * g + kt - 1)
                    for c in range(C):
                        last = nc.tensor.matmul(banks[kt % 2][:, c * CH:(c + 1) * CH], ks[:, bass.ds(h * S + kt * P, P)],
                                                qs[:, bass.ds(h * S + c * CH, CH)], start=True, stop=True)
                    last.then_inc(scored, 1)

                def values(h, par, hh, kt):
                    g = b * HA + h
                    acc = banks[2 + par]
                    pe.wait_ge(masked, 8 * g + kt + 1)
                    if kt == 0:
                        pe.wait_ge(vh_ready, g + 1)
                        pe.wait_ge(normed[par], 1 + b * (HA // 2) + hh)
                    for c in range(C):
                        rows = acc[32 * c:32 * c + 32, :]
                        dc = kt - c * (CH // P)
                        if 0 <= dc < CH // P:
                            nc.tensor.matmul(rows[:, dc * P:(dc + 1) * P], vh[:, par, kt, :], diag[:, kt % 2, :],
                                             start=(kt == 0), stop=False, skip_group_check=True)
                        q0 = max(0, (dc + 1) * P)
                        if q0 < CH:
                            nc.tensor.matmul(rows[:, q0:CH], vh[:, par, kt, :], prob[:, kt % 4, c * CH + q0:(c + 1) * CH],
                                             start=(kt == 0 and c > 0), stop=False, skip_group_check=True)
                    for c in range(C):
                        last = nc.tensor.matmul(acc[64 + 32 * c:96 + 32 * c, 0:CH], ones[:, :],
                                                prob[:, kt % 4, c * CH:(c + 1) * CH],
                                                start=(kt == 0), stop=(kt == T - 1), skip_group_check=True)
                    last.then_inc(summed, 1)

                def pair(hh, last):
                    for par in range(2):
                        h = 2 * hh + par
                        for kt in range(T):
                            if kt + 2 < T:
                                score(h, kt + 2)
                            elif not (last and par == 1):
                                score(h + 1, kt + 2 - T)
                            values(h, par, hh, kt)

                pe.wait_ge(m_in, 16 * b + 16)
                score(0, 0, first=True)
                score(0, 1, first=True)
                with pe.Fori(0, HA // 2 - 1) as hh:
                    pair(hh, False)
                pair(HA // 2 - 1, True)


def branch_b(nc, x, w_pair, w_oB, w_1, w_2, par_d, cB, cM, w_oA, xnt_scr, o_scr, rinv_scr, out):
    with ExitStack() as ctx:
        sb = lambda n, s, d=F32: ctx.enter_context(nc.sbuf_tensor(n, s, d))
        ps = lambda n: ctx.enter_context(nc.psum_tensor(n, [P, S], F32))
        sem = lambda n: ctx.enter_context(nc.semaphore(n))
        base = sb("base", [P, 4, S])
        table = sb("table", [P, 4, S])
        consts = sb("consts", [P, CONSTS])
        ident, mean_w = (consts[:, i * P:(i + 1) * P] for i in range(2))
        headsum = consts[:, 2 * P:2 * P + 32]
        cmask = consts[:, 2 * P + 32:2 * P + 32 + 3 * SPAN].rearrange("p (m n) -> p m n", m=3)
        mask = sb("mask", [P, 3, 2, SPAN], BF16)
        identb = sb("identb", [P, P], BF16)
        onesb = sb("onesb", [P, P], BF16)
        zerob = sb("zerob", [P, P], BF16)
        wo_a = sb("wo_a", [P, D])
        wqk, wv, wo = sb("wqk", [P, 2 * P]), sb("wv", [P, P]), sb("wo", [P, D])
        w1, w2 = sb("w1", [P, 2 * DIP]), sb("w2", [P, NJ, D])
        scales, par = sb("scales", [P, 4]), sb("par", [P, 9])
        xa, xb = sb("xa", [P, S + 1]), sb("xb", [P, S + 1])
        raw_swp = sb("raw_swp", [P, 8, CH])
        raw, swp = raw_swp[:, 0:4, :], raw_swp[:, 4:8, :]
        rcos, rsin, rsum, sq, rinv = (sb(n, [P, 4, CH]) for n in ("rcos", "rsin", "rsum", "sq", "rinv"))
        ssq, lnss, rinvc = (sb(n, [P, CH]) for n in ("ssq", "lnss", "rinvc"))
        qp = sb("qp", [P, 2, S + WIN])
        kk = sb("kk", [P, S])
        qpb = sb("qpb", [P, 2, S + WIN], BF16)
        kb = sb("kb", [P, WIN + S], BF16)
        negm = sb("negm", [P, T, 2])
        dm = sb("dm", [P, 2, S + WIN], BF16)
        va = sb("va", [P, T, 2, P])
        vnext = sb("vnext", [P, T, P])
        prob = sb("prob", [P, T, 2, SPAN])
        rec, lnden, ot = sb("rec", [P, 2, CH]), sb("lnden", [P, 2, CH]), sb("ot", [P, S])
        xcen, xsq, lnvar, rstd, xm, xnn = (t[:, 0:C, :].rearrange("p c n -> p (c n)")
                                           for t in (rcos, sq, raw, swp, rsin, rsum))
        hid = raw_swp[:, 0:NJ * C, :].rearrange("p (j c) n -> p j (c n)", j=NJ)
        gate = sb("gate", [P, 2, CH])
        xtok, oa, yout = sb("xtok", [P, T, D]), sb("oa", [P, S]), sb("yout", [P, T, D])
        epsc = sb("epsc", [P, 2])
        pq, pS, po, py = (ps(n) for n in ("pq", "pS", "po", "py"))
        bank = lambda t, i: t[:, i * CH:(i + 1) * CH]

        const_in, base_in, woa_in = sem("const_in"), sem("base_in"), sem("woa_in")
        pool_init, dve_init = sem("pool_init"), sem("dve_init")
        wqk_in, wv_in, wo_in, ffw_in = sem("wqk_in"), sem("wv_in"), sem("wo_in"), sem("ffw_in")
        scales_in, xs_in, xtok_in, oa_in = sem("scales_in"), sem("xs_in"), sem("xtok_in"), sem("oa_in")
        table_ready = sem("table_ready")
        filled = sem("filled")
        dve_read, act_read = sem("dve_read"), sem("act_read")
        raw_ready, swapped, rotated = sem("raw_ready"), sem("swapped"), sem("rotated")
        rinvc_ready, rinv_out, rinv_in = sem("rinvc_ready"), sem("rinv_out"), sem("rinv_in")
        rot_sum = sem("rot_sum")
        ln_done = sem("ln_done")
        v_placed = sem("v_placed")
        qk_ready = sem("qk_ready")
        bf_ready = sem("bf_ready")
        guard, negm_ready, diag_ready = sem("guard"), sem("negm_ready"), sem("diag_ready")
        rec_ready, lnden_done = sem("rec_ready"), sem("lnden_done")
        scored, exped, valued = sem("scored"), sem("exped"), sem("valued")
        o_ready, wo_done = sem("o_ready"), sem("wo_done")
        xa_ready, xb_ready = sem("xa_ready"), sem("xb_ready")
        f_mean, f_cen, f_sq, f_var = sem("f_mean"), sem("f_cen"), sem("f_sq"), sem("f_var")
        f_ln, f_rstd, f_xm, f_xn = sem("f_ln"), sem("f_rstd"), sem("f_xm"), sem("f_xn")
        f_up, f_gate, f_hid, f_down = sem("f_up"), sem("f_gate"), sem("f_hid"), sem("f_down")
        f_py = sem("f_py")
        k_sum = sem("k_sum")
        straight, fin, fin_sum, out_saved = sem("straight"), sem("fin"), sem("fin_sum"), sem("out_saved")
        block = ctx.enter_context(nc.Block())
        proj_bank = lambda n: bank((pq, po)[n // 2], n % 2)
        QK_BLOCKS = [(0, 0, 64), (1, 64, 128)]

        def units(eng, first, second, middle, last, before, after, batch_start, batch_end):
            with eng.Fori(0, B) as b:
                batch_start(b)
                with eng.Fori(0, L) as l:
                    f = b * L + l
                    before(b, l, f)
                    first(f, f * NP, l)
                    second(f * NP + 1)
                    with eng.Fori(2, NP) as i:
                        middle(f * NP + i)
                    last(f, f * NP + NP, l)
                    after(b, l, f)
                batch_end(b)

        @block.sync
        def _(sp):
            for started in (out_saved, swapped, rinv_in):
                sp.nop().then_inc(started, 1)
            sp.dma_start(consts[:, :], cM).then_inc(const_in, 16)
            sp.dma_start(base[:, :, :], cB).then_inc(base_in, 16)
            sp.dma_start(wo_a[:, :], w_oA).then_inc(woa_in, 16)
            sp.dma_start(scales[:, :], par_d[0, :, 0:4]).then_inc(scales_in, 16)

            def load_qk(pair):
                sp.dma_start(wqk[:, :], w_pair[pair, :, 0:2 * P]).then_inc(wqk_in, 16)

            def load_v(pair):
                sp.dma_start(wv[:, :], w_pair[pair, :, 2 * P:3 * P]).then_inc(wv_in, 16)

            def load_wo(v, pair):
                sp.wait_ge(wo_done, 1 + v)
                sp.dma_start(wo[:, :], w_oB[pair]).then_inc(wo_in, 16)

            def swap(u):
                sp.wait_ge(raw_ready, 4 * u + 4)
                for a in range(4):
                    sp.dma_start(swp[32 * (a ^ 1):32 * (a ^ 1) + 32, :, :], raw[32 * a:32 * a + 32, :, :]).then_inc(swapped, 16)

            def spread(u):
                sp.wait_ge(rinvc_ready, u + 1)
                sp.dma_start(rinv_scr, rinvc[0:7 * 16 + 1:16, :]).then_inc(rinv_out, 16)
                sp.wait_ge(rinv_out, 16 * u + 16)
                for h in range(2):
                    src = rinv_scr.rearrange("(o j h) n -> o h j n", o=1, h=2)[:, h]
                    sp.dma_start(rinv[64 * h:64 * h + 64, :, :], src.broadcast_to([64, 4, CH])).then_inc(rinv_in, 16)

            with sp.Fori(0, B) as b:
                sp.wait_ge(fin, 1 + b)
                for lo, hi, off in ((0, 64, 0), (64, 128, 1)):
                    sp.dma_start(xa[lo:hi, off:off + S], xnt_scr[b, lo:hi, :]).then_inc(xs_in, 16)
                sp.dma_start(oa[:, :], o_scr[b]).then_inc(oa_in, 16)
                sp.wait_ge(fin_sum, 1 + b)
                sp.dma_start(xtok[:, :, :], x[b].rearrange("(t p) d -> p t d", p=P)).then_inc(xtok_in, 16)
                with sp.Fori(0, L) as l:
                    f = b * L + l
                    u = f * NP
                    sp.wait_ge(wo_done, 1 + u)
                    load_qk(l * NP)
                    load_v(l * NP)
                    swap(u)
                    load_qk(l * NP + 1)
                    spread(u)
                    sp.wait_ge(table_ready, 1 + 4 * f + 4)
                    sp.dma_start(scales[:, :], par_d[l + 1, :, 0:4]).then_inc(scales_in, 16)
                    sp.wait_ge(filled, 1 + ITEMS * u + ITEMS)
                    load_v(l * NP + 1)
                    sp.dma_start(par[:, :], par_d[l, :, 4:13]).then_inc(ffw_in, 16)
                    sp.dma_start(w1[:, :], w_1[l]).then_inc(ffw_in, 16)
                    sp.dma_start(w2[:, :, :], w_2[l].rearrange("(j p) d -> p j d", p=P)).then_inc(ffw_in, 16)
                    with sp.Fori(1, NP - 1) as i:
                        swap(u + i)
                        load_qk(l * NP + i + 1)
                        spread(u + i)
                        load_wo(u + i - 1, l * NP + i - 1)
                        sp.wait_ge(filled, 1 + ITEMS * (u + i) + ITEMS)
                        load_v(l * NP + i + 1)
                    swap(u + NP - 1)
                    spread(u + NP - 1)
                    load_wo(u + NP - 2, l * NP + NP - 2)
                    load_wo(u + NP - 1, l * NP + NP - 1)
                sp.wait_ge(fin_sum, 1 + b + 1)
                sp.dma_start(out[b].rearrange("(t p) d -> p t d", p=P), yout[:, :, :]).then_inc(out_saved, 16)
            sp.wait_ge(out_saved, 1 + 16 * B)

        @block.gpsimd
        def _(pool):
            for started in (rot_sum, v_placed):
                pool.nop().then_inc(started, 1)
            for t in (qp, qpb, dm):
                nc.gpsimd.memset(t[:, :, :], 0.0)
            nc.gpsimd.memset(kb[:, 0:WIN], 0.0)
            nc.gpsimd.memset(va[:, :, :, :], 1.0)
            nc.gpsimd.memset(onesb[:, :], 1.0)
            nc.gpsimd.memset(epsc[:, 0:1], EPS)
            nc.gpsimd.memset(epsc[:, 1:2], 12.0 * float(np.log(2.0)))
            nc.gpsimd.memset(zerob[:, :], 0.0).then_inc(pool_init, 1)
            pool.wait_ge(pool_init, 1)

            def add_rotated(u, items=(0, 1, 2, 3)):
                for j in items:
                    pool.wait_ge(rotated, 1 + 8 * u + 4 + j + 1)
                    if j == 0:
                        pool.wait_ge(qk_ready, 1 + 6 * u)
                    nc.gpsimd.tensor_tensor(rsum[:, j, :], rcos[:, j, :], rsin[:, j, :],
                                            ALU.add).then_inc(rot_sum, 4 // len(items))

            def diagonals(v):
                for part in range(2):
                    tiles = slice(part * T // 2, (part + 1) * T // 2)
                    pool.wait_ge(negm_ready, T * v + (part + 1) * T // 2)
                    if part == 0:
                        pool.wait_ge(dve_init, 1)
                    for h in range(2):
                        nc.gpsimd.tensor_tensor(dm[:, h, part * CH:(part + 1) * CH].rearrange("p (t n) -> p t n", n=P),
                                                identb[:, :].rearrange("p (o n) -> p o n", o=1).broadcast_to([P, T // 2, P]),
                                                negm[:, tiles, h:h + 1].broadcast_to([P, T // 2, P]),
                                                ALU.mult).then_inc(diag_ready, 1)

            def place_v(u):
                pool.wait_ge(act_read, 1 + ACT_ITEMS * u + ACT_ITEMS)
                for h in range(2):
                    if h == 0:
                        pool.wait_ge(valued, 1 + 2 * u)
                    ins = nc.gpsimd.tensor_tensor(va[:, :, h, h * DB:(h + 1) * DB], vnext[:, :, h * DB:(h + 1) * DB],
                                                  onesb[:, 0:DB].rearrange("p (o n) -> p o n", o=1).broadcast_to([P, T, DB]),
                                                  ALU.mult)
                ins.then_inc(v_placed, 1)

            def first(f, u, l):
                add_rotated(u, (0, 2))
                place_v(u)

            def middle(u):
                diagonals(u - 1)
                add_rotated(u)
                place_v(u)

            none = lambda b: None
            units(pool, first, middle, middle, lambda f, u, l: diagonals(u - 1), lambda b, l, f: None, lambda b, l, f: None, none, none)

        @block.vector
        def _(dve):
            for started in (fin_sum, dve_read, o_ready, qk_ready, rotated):
                dve.nop().then_inc(started, 1)
            dve.nop().then_inc(xa_ready, C)
            dve.wait_ge(const_in, 16)
            nc.vector.memset(xa[64:128, 0:1], 0.0)
            nc.vector.memset(xb[64:128, 0:1], 0.0)
            nc.vector.tensor_copy(identb[:, :], ident)
            nc.vector.tensor_copy(mask[:, :, 0, :], cmask)
            nc.vector.tensor_copy(mask[:, :, 1, :], cmask).then_inc(dve_init, 1)

            def rotate(u, which, start=None):
                if start is not None:
                    dve.wait_ge(table_ready, 1 + 4 * start + 4)
                src, dst = ((raw, rcos), (swp, rsin))[which]
                for j in range(4):
                    if which == 0:
                        dve.wait_ge(raw_ready, 4 * u + j + 1)
                        if j == 0:
                            dve.wait_ge(rot_sum, 1 + 4 * u)
                    elif j == 0:
                        dve.wait_ge(swapped, 1 + 64 * u + 64)
                    k, c = j % 2, j // 2
                    nc.vector.tensor_tensor(dst[:, j, :], src[:, j, :], table[:, 2 * k + which, c * CH:(c + 1) * CH],
                                            ALU.mult).then_inc(rotated, 1)

            def maxima(v):
                for qt in range(T):
                    dve.wait_ge(guard, T * v + qt + 1)
                    nc.vector.tensor_reduce(negm[:, qt, :], bank(pS, qt % 2)[:, 0:2 * SPAN].rearrange("p (h n) -> p h n", h=2),
                                            axis=AX.X, op=ALU.max, negate=True).then_inc(negm_ready, 1)

            def divide(v, half):
                src = (pq, po)[half]
                cols = slice(half * CH, (half + 1) * CH)
                dve.wait_ge(rec_ready, 2 * v + half + 1)
                nc.vector.tensor_tensor(ot[0:64, cols], src[0:64, 0:CH], rec[0:64, half, :], ALU.mult)
                nc.vector.tensor_tensor(ot[64:128, cols], src[64:128, CH:2 * CH], rec[64:128, half, :],
                                        ALU.mult).then_inc(o_ready, 1)

            def add_k(u, f):
                dve.wait_ge(rotated, 1 + 8 * u + 8)
                for j in (1, 3):
                    nc.vector.tensor_tensor(rsum[:, j, :], rcos[:, j, :], rsin[:, j, :], ALU.add).then_inc(k_sum, 1)
                dve.wait_ge(k_sum, 2 * f + 2)

            def normalise(u, items, k_added=False):
                for j in items:
                    c = j // 2
                    if j == 1:
                        dve.wait_ge(rinv_in, 1 + 16 * BCAST * (u + 1))
                        dve.wait_ge(scored, 1 + T * u)
                    if j == (0 if k_added else 1):
                        dve.wait_ge(rot_sum, 1 + 4 * u + 4)
                    if j % 2 == 0:
                        for h, lo, hi in QK_BLOCKS:
                            nc.vector.tensor_tensor(qp[lo:hi, h, c * CH:(c + 1) * CH], rsum[lo:hi, j, :],
                                                    rinv[lo:hi, j, :], ALU.mult).then_inc(qk_ready, 1)
                    else:
                        nc.vector.tensor_tensor(kk[:, c * CH:(c + 1) * CH], rsum[:, j, :], rinv[:, j, :],
                                                ALU.mult).then_inc(qk_ready, 1)

            def clamp(u):
                dve.wait_ge(filled, 1 + ITEMS * u + 5)
                nc.vector.tensor_scalar(ssq[:, :], bank(po, 0), 1e-24, None, ALU.max).then_inc(dve_read, 1)

            def first(f, u, l):
                rotate(u, 0, f)
                clamp(u)
                rotate(u, 1)
                add_k(u, f)
                normalise(u, (1, 3, 0, 2), k_added=True)

            def middle(u):
                maxima(u - 1)
                clamp(u)
                rotate(u, 0)
                rotate(u, 1)
                divide(u - 1, 0)
                normalise(u, (1, 3, 0))
                divide(u - 1, 1)
                normalise(u, (2,))

            def mid_stream(f, c):
                if c == 0:
                    dve.wait_ge(f_py, f + 1)
                else:
                    dve.wait_ge(wo_done, 1 + NP * f + NP)
                for lo, hi, off in ((0, 64, 0), (64, 128, 1)):
                    cols = slice(c * CH + off, (c + 1) * CH + off)
                    ins = nc.vector.tensor_tensor(xb[lo:hi, cols], py[lo:hi, c * CH:(c + 1) * CH], xa[lo:hi, cols], ALU.add)
                ins.then_inc(xb_ready, 1)

            def centre(f, c):
                dve.wait_ge(xb_ready, C * f + c + 1)
                dve.wait_ge(f_mean, C * f + c + 1)
                nc.vector.tensor_tensor(xcen[:, c * CH:(c + 1) * CH], xb[:, c * CH:(c + 1) * CH], bank(pq, c),
                                        ALU.subtract).then_inc(f_cen, 1)

            def last(f, u, l):
                maxima(u - 1)
                divide(u - 1, 0)
                mid_stream(f, 0)
                divide(u - 1, 1)

            def after(b, l, f):
                centre(f, 0)
                mid_stream(f, 1)
                centre(f, 1)
                for c in range(C):
                    dve.wait_ge(f_rstd, C * f + c + 1)
                    if c == 0:
                        dve.wait_ge(f_cen, C * f + C)
                    nc.vector.tensor_tensor(xm[:, c * CH:(c + 1) * CH], xcen[:, c * CH:(c + 1) * CH],
                                            rstd[:, c * CH:(c + 1) * CH], ALU.mult).then_inc(f_xm, 1)

                def hidden(n):
                    c, j = n // NJ, n % NJ
                    dve.wait_ge(f_gate, C * NJ * f + n + 1)
                    nc.vector.scalar_tensor_tensor(hid[:, j, c * CH:(c + 1) * CH], (pq, pS)[n % 2][:, 0:CH],
                                                   par[:, 2 + j:3 + j], gate[:, n % 2, :], ALU.add, ALU.mult).then_inc(f_hid, 1)

                def next_stream(c):
                    dve.wait_ge(f_down, C * f + c + 1)
                    for lo, hi, off in ((0, 64, 0), (64, 128, 1)):
                        cols = slice(c * CH + off, (c + 1) * CH + off)
                        ins = nc.vector.scalar_tensor_tensor(xa[lo:hi, cols], py[lo:hi, c * CH:(c + 1) * CH],
                                                             par[lo:hi, 8:9], xb[lo:hi, cols], ALU.add, ALU.add)
                    ins.then_inc(xa_ready, 1)

                for n in range(C * NJ - 1):
                    hidden(n)
                next_stream(0)
                hidden(C * NJ - 1)
                next_stream(1)

            def batch_end(b):
                dve.wait_ge(xa_ready, C + C * (L * b + L))
                for lo, hi, off in ((0, 64, 0), (64, 128, 1)):
                    ins = nc.vector.tensor_copy(ot[lo:hi, :], xa[lo:hi, off:off + S])
                ins.then_inc(straight, 1)
                dve.wait_ge(fin, 1 + b + 1)
                dve.wait_ge(xtok_in, 16 * b + 16)
                dve.wait_ge(out_saved, 1 + 16 * b)
                nc.vector.tensor_tensor(yout[:, :, :], pq[:, :].rearrange("p (t d) -> p t d", t=T), xtok[:, :, :],
                                        ALU.add).then_inc(fin_sum, 1)

            units(dve, first, middle, middle, last, lambda b, l, f: None, after, lambda b: None, batch_end)

        @block.scalar
        def _(act):
            for started in (table_ready, act_read,):
                act.nop().then_inc(started, 1)
            act.wait_ge(pool_init, 1)

            def take_qk(u):
                for j in range(4):
                    act.wait_ge(filled, 1 + ITEMS * u + j + 1)
                    if j == 0:
                        act.wait_ge(swapped, 1 + 64 * u)
                        act.wait_ge(rotated, 1 + 8 * u)
                    nc.scalar.activation(raw[:, j, :], proj_bank(j), ACT.Copy).then_inc(raw_ready, 1)
                    nc.scalar.activation(sq[:, j, :], proj_bank(j), ACT.Square).then_inc(act_read, 1)

            def round_qk(u):
                act.wait_ge(qk_ready, 1 + 6 * u + 2)
                nc.scalar.activation(kb[:, WIN:WIN + S], kk[:, :], ACT.Copy).then_inc(bf_ready, 1)
                for c in range(C):
                    act.wait_ge(qk_ready, 1 + 6 * u + 4 + 2 * c)
                    for h, lo, hi in QK_BLOCKS:
                        ins = nc.scalar.activation(qpb[lo:hi, h, c * CH:(c + 1) * CH], qp[lo:hi, h, c * CH:(c + 1) * CH], ACT.Copy)
                    ins.then_inc(bf_ready, 1)

            def exps(v, kts):
                for kt in kts:
                    act.wait_ge(scored, 1 + T * v + kt + 1)
                    nc.scalar.activation(prob[:, kt, :, :], bank(pS, kt % 2)[:, 0:2 * SPAN].rearrange("p (h n) -> p h n", h=2),
                                         ACT.Exp).then_inc(exped, 1)

            def invert(v, half):
                src = (pq, po)[half]
                act.wait_ge(valued, 1 + 2 * v + half + 1)
                nc.scalar.activation(lnden[0:64, half, :], src[64:128, 0:CH], ACT.Ln)
                nc.scalar.activation(lnden[64:128, half, :], src[0:64, CH:2 * CH], ACT.Ln).then_inc(lnden_done, 1)
                act.wait_ge(lnden_done, 2 * v + half + 1)
                nc.scalar.activation(rec[:, half, :], lnden[:, half, :], ACT.Exp, scale=-1.0).then_inc(rec_ready, 1)

            def norms(u):
                act.wait_ge(dve_read, 1 + u + 1)
                nc.scalar.activation(lnss[:, :], ssq[:, :], ACT.Ln, scale=2.0 ** 24).then_inc(ln_done, 1)
                act.wait_ge(ln_done, u + 1)
                nc.scalar.activation(rinvc[:, :], lnss[:, :], ACT.Exp, scale=-0.5, bias=epsc[:, 1:2]).then_inc(rinvc_ready, 1)

            def take_v(u):
                for n in range(2):
                    act.wait_ge(filled, 1 + ITEMS * u + 5 + n + 1)
                    if n == 0:
                        act.wait_ge(v_placed, 1 + u)
                    nc.scalar.activation(vnext[:, 4 * n:4 * n + 4, :], bank(pq, n).rearrange("p (t d) -> p t d", t=4),
                                         ACT.Copy).then_inc(act_read, 1)

            def first(f, u, l):
                take_qk(u)
                norms(u)
                take_v(u)
                round_qk(u)

            def middle(u):
                take_qk(u)
                norms(u)
                take_v(u)
                exps(u - 1, range(6))
                invert(u - 1, 0)
                exps(u - 1, range(6, T))
                invert(u - 1, 1)
                round_qk(u)

            def last(f, u, l):
                next_table(f + 1)
                exps(u - 1, range(6))
                invert(u - 1, 0)
                exps(u - 1, range(6, T))
                invert(u - 1, 1)

            def after(b, l, f):
                def square(c):
                    act.wait_ge(f_cen, C * f + c + 1)
                    nc.scalar.activation(xsq[:, c * CH:(c + 1) * CH], xcen[:, c * CH:(c + 1) * CH], ACT.Square).then_inc(f_sq, 1)

                def inverse_deviation(c):
                    act.wait_ge(f_var, C * f + c + 1)
                    nc.scalar.activation(lnvar[:, c * CH:(c + 1) * CH], bank(pS, c), ACT.Ln, bias=epsc[:, 0:1]).then_inc(f_ln, 1)
                    act.wait_ge(f_ln, C * f + c + 1)
                    nc.scalar.activation(rstd[:, c * CH:(c + 1) * CH], lnvar[:, c * CH:(c + 1) * CH], ACT.Exp,
                                         scale=-0.5).then_inc(f_rstd, 1)

                def gain(c):
                    act.wait_ge(f_xm, C * f + c + 1)
                    if c == 0:
                        act.wait_ge(ffw_in, 48 * f + 48)
                    nc.scalar.activation(xnn[:, c * CH:(c + 1) * CH], xm[:, c * CH:(c + 1) * CH], ACT.Identity,
                                         scale=par[:, 0:1], bias=par[:, 1:2]).then_inc(f_xn, 1)

                square(0)
                inverse_deviation(0)
                square(1)
                gain(0)
                inverse_deviation(1)
                gain(1)
                for n in range(C * NJ):
                    j = n % NJ
                    act.wait_ge(f_up, C * NJ * f + n + 1)
                    nc.scalar.activation(gate[:, n % 2, :], (pq, pS)[n % 2][:, CH:2 * CH], ACT.Gelu,
                                         bias=par[:, 5 + j:6 + j]).then_inc(f_gate, 1)

            def before(b, l, f):
                nc.scalar.preload_act_table_set(EXP_LN_SET)

            def next_table(f):
                act.wait_ge(base_in, 16)
                act.wait_ge(scales_in, 16 * f + 16)
                act.wait_ge(rotated, 1 + 8 * NP * f)
                for k in range(4):
                    nc.scalar.activation(table[:, k, :], base[:, k, :], ACT.Copy, scale=scales[:, k:k + 1]).then_inc(table_ready, 1)

            next_table(0)
            units(act, first, middle, middle, last, before, after, lambda b: None, lambda b: None)

        @block.tensor
        def _(pe):
            for started in (fin, filled, wo_done, scored, valued):
                pe.nop().then_inc(started, 1)
            pe.wait_ge(pool_init, 1)
            pe.wait_ge(dve_init, 1)
            pe.wait_ge(const_in, 16)
            pe.wait_ge(woa_in, 16)

            def project_qk(u, chunk):
                if chunk == 0:
                    pe.wait_ge(wqk_in, 16 * u + 16)
                for k in range(2):
                    nc.tensor.matmul(proj_bank(2 * chunk + k), wqk[:, k * P:(k + 1) * P],
                                     xa[:, chunk * CH:(chunk + 1) * CH], start=True, stop=True).then_inc(filled, 1)

            def norms(u):
                pe.wait_ge(act_read, 1 + ACT_ITEMS * u + 4)
                for j in range(4):
                    last = nc.tensor.matmul(po[32 * j:32 * j + 32, 0:CH], headsum, sq[:, j, :], start=True, stop=True,
                                            skip_group_check=True)
                last.then_inc(filled, 1)

            def project_v(u):
                pe.wait_ge(wv_in, 16 * u + 16)
                for n in range(2):
                    for t in range(4):
                        tt = 4 * n + t
                        last = nc.tensor.matmul(bank(pq, n)[:, t * P:(t + 1) * P], xa[:, tt * P:(tt + 1) * P], wv[:, :],
                                                start=True, stop=True)
                    last.then_inc(filled, 1)

            def maxima(v):
                for qt in range(T):
                    if qt % 4 == 0:
                        pe.wait_ge(bf_ready, 3 * v + 2 + qt // 4)
                    if qt >= 2:
                        pe.wait_ge(negm_ready, T * v + qt - 1)
                    dst = bank(pS, qt % 2)
                    for h in range(2):
                        nc.tensor.matmul(dst[:, h * SPAN:(h + 1) * SPAN], qpb[:, h, qt * P:(qt + 1) * P],
                                         kb[:, qt * P:qt * P + SPAN], start=(h == 0), stop=False, skip_group_check=True)
                    nc.tensor.matmul(dst[:, 0:2 * SPAN], identb[:, :], mask[:, 2 if qt == 0 else 1, :, :],
                                     start=False, stop=True, skip_group_check=True).then_inc(guard, 1)

            def attend(v, pq_free, po_free):
                def score(kt):
                    if kt < 2:
                        pe.wait_ge(negm_ready, T * v + T - 1 + kt)
                    else:
                        pe.wait_ge(exped, T * v + kt - 1)
                    dst = bank(pS, kt % 2)[:, 0:2 * SPAN]
                    nc.tensor.matmul(dst, kk[:, kt * P:(kt + 1) * P], qp[:, :, kt * P:kt * P + SPAN],
                                     start=True, stop=False)
                    nc.tensor.matmul(dst, identb[:, :], mask[:, 0, :, :], start=False, stop=False)
                    if kt in (0, 3):
                        pe.wait_ge(diag_ready, 4 * v + (2 if kt == 0 else 4))
                    nc.tensor.matmul(dst, onesb[:, :], dm[:, :, kt * P:kt * P + SPAN], start=False,
                                     stop=True).then_inc(scored, 1)

                def values(kt):
                    pe.wait_ge(exped, T * v + kt + 1)
                    if kt == 0:
                        pe.wait_ge(v_placed, 1 + v + 1)
                        pq_free()
                    if kt == 3:
                        po_free()
                    for half, dst in ((0, pq), (1, po)):
                        lo, hi = max(kt * P, half * CH), min(kt * P + SPAN, (half + 1) * CH)
                        if lo >= hi:
                            continue
                        for h in range(2):
                            last = nc.tensor.matmul(bank(dst, h)[:, lo - half * CH:hi - half * CH], va[:, kt, h, :],
                                                    prob[:, kt, h, lo - kt * P:hi - kt * P],
                                                    start=(kt == (0, 3)[half]), stop=False, skip_group_check=True)
                        if (half, kt) in ((0, 3), (1, 7)):
                            last.then_inc(valued, 1)

                score(0)
                for kt in range(T):
                    if kt + 1 < T:
                        score(kt + 1)
                    values(kt)

            def project_out(v, chunks=range(C), last_of_phase=False):
                for c in chunks:
                    pe.wait_ge(o_ready, 1 + 2 * v + c + 1)
                    if c == 0:
                        pe.wait_ge(wo_in, 16 * v + 16)
                    last = nc.tensor.matmul(bank(py, c), wo[:, :], ot[:, c * CH:(c + 1) * CH], start=False, stop=False,
                                            skip_group_check=True)
                    if c == C - 1:
                        last.then_inc(wo_done, 1)
                    elif last_of_phase:
                        last.then_inc(f_py, 1)

            def batch_start(b):
                pass

            def before(b, l, f):
                pe.wait_ge(xs_in, 32 * b + 32)
                pe.wait_ge(fin_sum, 1 + b)

            def clear(f, c):
                pe.wait_ge(xa_ready, C * f + c + 1)
                nc.tensor.matmul(bank(py, c)[:, 0:2 * SPAN], zerob[:, :], mask[:, 0, :, :], start=True, stop=False,
                                 skip_group_check=True)
                nc.tensor.matmul(bank(py, c)[:, 2 * SPAN:CH], zerob[:, :], dm[:, 0, 0:CH - 2 * SPAN], start=False,
                                 stop=False, skip_group_check=True)

            def first(f, u, l):
                for c in range(C):
                    clear(f, c)
                    project_qk(u, c)
                norms(u)
                project_v(u)

            def second(u):
                pe.wait_ge(act_read, 1 + ACT_ITEMS * u)
                project_qk(u, 0)
                pe.wait_ge(dve_read, 1 + u)
                project_qk(u, 1)
                rest(u)

            def middle(u):
                pe.wait_ge(o_ready, 1 + 2 * (u - 2) + 1)
                project_qk(u, 0)
                project_out(u - 2)
                project_qk(u, 1)
                rest(u)

            def rest(u):
                maxima(u - 1)
                norms(u)
                project_v(u)
                attend(u - 1, lambda: pe.wait_ge(act_read, 1 + ACT_ITEMS * u + ACT_ITEMS),
                       lambda: pe.wait_ge(dve_read, 1 + u + 1))

            def mean(f, c):
                pe.wait_ge(xb_ready, C * f + c + 1)
                nc.tensor.matmul(bank(pq, c), mean_w, xb[:, c * CH:(c + 1) * CH], start=True, stop=True).then_inc(f_mean, 1)

            def variance(f, c):
                pe.wait_ge(f_sq, C * f + c + 1)
                nc.tensor.matmul(bank(pS, c), mean_w, xsq[:, c * CH:(c + 1) * CH], start=True, stop=True).then_inc(f_var, 1)

            def last(f, u, l):
                project_out(u - 2)
                maxima(u - 1)
                attend(u - 1, lambda: None, lambda: None)
                project_out(u - 1, (0,), last_of_phase=True)
                mean(f, 0)
                project_out(u - 1, (1,))

            def after(b, l, f):
                variance(f, 0)
                mean(f, 1)
                variance(f, 1)

                def up(n):
                    c, j = n // NJ, n % NJ
                    if j == 0:
                        pe.wait_ge(f_xn, C * f + c + 1)
                    if n == 0:
                        pe.wait_ge(f_cen, C * f + C)
                        pe.wait_ge(ffw_in, 48 * f + 48)
                    elif n == 1:
                        pe.wait_ge(f_ln, C * f + C)
                    else:
                        pe.wait_ge(f_hid, C * NJ * f + n - 1)
                    for k in range(2):
                        last = nc.tensor.matmul((pq, pS)[n % 2][:, k * CH:(k + 1) * CH],
                                                w1[:, k * DIP + j * P:k * DIP + (j + 1) * P],
                                                xnn[:, c * CH:(c + 1) * CH], start=True, stop=True)
                    last.then_inc(f_up, 1)

                def down(c):
                    for j in range(NJ):
                        pe.wait_ge(f_hid, C * NJ * f + c * NJ + j + 1)
                        last = nc.tensor.matmul(bank(py, c), w2[:, j, :], hid[:, j, c * CH:(c + 1) * CH],
                                                start=(j == 0), stop=(j == NJ - 1))
                    last.then_inc(f_down, 1)

                for n in range(C * NJ - 1):
                    up(n)
                down(0)
                up(C * NJ - 1)
                down(1)

            def batch_end(b):
                pe.wait_ge(straight, b + 1)
                pe.wait_ge(oa_in, 16 * b + 16)
                for t in range(T):
                    dst = pq[:, t * P:(t + 1) * P]
                    nc.tensor.matmul(dst, oa[:, t * P:(t + 1) * P], wo_a[:, :], start=(t % 4 == 0), stop=False,
                                     skip_group_check=True)
                    last = nc.tensor.matmul(dst, ot[:, t * P:(t + 1) * P], ident, start=False, stop=False,
                                            skip_group_check=True)
                last.then_inc(fin, 1)

            units(pe, first, second, middle, last, before, after, batch_start, batch_end)


def build(nc, a, out):
    o_scr = nc.dram_tensor("o_scr", (B, D, S), F32).ap()
    xnt_scr = nc.dram_tensor("xnt_scr", (B, D, S), F32).ap()
    part_scr = nc.dram_tensor("part_scr", (2, 3, D, S), BF16).ap()
    m_scr = nc.dram_tensor("m_scr", (P, P), BF16).ap()
    rinv_scr = nc.dram_tensor("rinv_scr", (8, CH), F32).ap()
    branch_a(nc, a["x"], a["wA"], a["cA"], a["cM"][:, 0:P], a["cM"][:, CONSTS - P:CONSTS], o_scr, xnt_scr, part_scr, m_scr)
    branch_b(nc, a["x"], a["w_pair"], a["w_oB"], a["w_1"], a["w_2"], a["par"], a["cB"], a["cM"], a["w_oA"],
             xnt_scr, o_scr, rinv_scr, out)


def position_constants():
    f = np.float32
    t = np.arange(S, dtype=f)
    inv = f(10000.0) ** (-(np.arange(DA // 2, dtype=f) * f(2.0) / f(DA)))
    ang = (t[:, None] * inv[None, :]).astype(f)
    d = np.arange(DA)
    sign = np.where(d % 2 == 0, f(-1), f(1))
    cA = np.stack([np.tile(np.cos(ang)[:, d // 2].T, (HA, 1)),
                   np.tile((np.sin(ang)[:, d // 2] * sign).T, (HA, 1))], 1).astype(f)
    half = np.arange(0, DB, 2, dtype=f)
    inv = (f(1.0) / f(10000.0) ** (half / f(DB))).astype(f)
    fr = (t[:, None] * inv[None, :]).astype(f)
    base = ((half + f(0.4 * DB)) / f(1.4 * DB)).astype(f)
    power = ((t - f(S // 2)) / f(WIN // 2)).astype(f)
    sc = (base[None, :] ** power[:, None]).astype(f)
    fr, sc = np.concatenate([fr, fr], -1), np.concatenate([sc, sc], -1)
    sign = np.where(np.arange(DB) < DB // 2, f(-1), f(1))[None, :]
    isc = (f(1.0) / sc).astype(f)
    tabs = [np.cos(fr) * sc * f(8), np.sin(fr) * sc * sign * f(8), np.cos(fr) * isc, np.sin(fr) * isc * sign]
    cB = np.stack([np.tile(x.T, (2, 1)) for x in tabs], 1).astype(f)
    p, n = np.arange(P)[:, None], np.arange(SPAN)[None, :]
    off = f(-1e30)
    by_key = np.where((n >= p) & (n <= p + WIN), f(0), off)
    by_query = by_key
    first = np.where(n < WIN, off, by_query)
    pair = (np.arange(P)[:, None] // DB == np.arange(32)[None, :] // 16).astype(f)
    cM = np.concatenate([np.eye(P, dtype=f), np.full((P, P), f(1.0 / D)), pair, by_key, by_query, first,
                         np.triu(np.ones((P, P), f))], 1).astype(f)
    return np.ascontiguousarray(cA), np.ascontiguousarray(cB), np.ascontiguousarray(cM)


def lay_out(i):
    c = np.ascontiguousarray
    swap = np.arange(D) ^ 1
    wq, wk, wv = (np.asarray(i[f"L0_attn_w_{n}"]).T for n in "qkv")
    wA = c(np.concatenate([wq, wq[:, swap], wk, wk[:, swap], wv], 1))
    W = np.asarray(i["L0_ffn_Wqkv"]).reshape(L, D, 3, NP, 2, DB)
    rot = np.concatenate([np.arange(DB // 2, DB), np.arange(DB // 2)])
    q, k, v = (W[:, :, n].transpose(0, 2, 1, 3, 4) for n in range(3))
    w_pair = c(np.stack([q, k, v], 3).reshape(L * NP, D, 3 * P))
    w_oB = c(np.asarray(i["L0_ffn_Wo"]).reshape(L * NP, P, D))
    pad = ((0, 0), (0, 0), (0, DIP - DI))
    W1 = np.asarray(i["L0_ffn_W1"])
    w_1 = c(np.concatenate([np.pad(W1[:, :, :DI], pad), np.pad(W1[:, :, DI:], pad)], 2))
    w_2 = c(np.pad(np.asarray(i["L0_ffn_W2"]), ((0, 0), (0, DIP - DI), (0, 0))))
    qs, ks = np.asarray(i["L0_ffn_q_scale"]), np.asarray(i["L0_ffn_k_scale"])
    two = lambda s: np.concatenate([s, s], 1)[:, :, None]
    b1 = np.asarray(i["L0_ffn_b1"])
    cols = lambda s: np.pad(s, ((0, 0), (0, DIP - DI))).reshape(L, NJ, P).transpose(0, 2, 1)
    par = c(np.concatenate([two(qs), two(qs[:, rot]), two(ks), two(ks[:, rot]),
                            np.asarray(i["L0_ffn_ln_g"])[:, :, None], np.asarray(i["L0_ffn_ln_b"])[:, :, None],
                            cols(b1[:, :DI]), cols(b1[:, DI:]), np.asarray(i["L0_ffn_b2"])[:, :, None]], 2))
    par = c(np.concatenate([par, par[:1]], 0))
    cA, cB, cM = position_constants()
    return {"x": c(np.asarray(i["L0_attn_x"])), "wA": wA, "w_oA": c(np.asarray(i["L0_attn_w_o"]).T), "w_pair": w_pair,
            "w_oB": w_oB, "w_1": w_1, "w_2": w_2, "par": par, "cA": cA, "cB": cB, "cM": cM}


def kernel(**inputs):
    import concourse.bacc as bacc
    from concourse.bass_utils import run_bass_kernel_spmd

    nc = bacc.Bacc("TRN2", target_bir_lowering=False, num_devices=1)
    arrays = lay_out(inputs)
    aps = {n: nc.dram_tensor(f"in_{n}", v.shape, mybir.dt.from_np(v.dtype), kind="ExternalInput").ap()
           for n, v in arrays.items()}
    out = nc.dram_tensor("out", (B, S, D), F32, kind="ExternalOutput").ap()
    build(nc, aps, out)
    r = run_bass_kernel_spmd(nc, [{f"in_{n}": v for n, v in arrays.items()}], core_ids=[0])
    return r.results[0]["out"]
```
